# Optimizing a Trainium2 kernel written in Bass

```python
import numpy as np
import jax
import jax.numpy as jnp

def _softmax(x, axis=-1):
    return jax.nn.softmax(x, axis=axis)

def _gelu(x):
    return jax.nn.gelu(x, approximate=True)

def _silu(x):
    return jax.nn.silu(x)

def _sigmoid(x):
    return jax.nn.sigmoid(x)

def _layernorm(x, axis=-1, eps=1e-05):
    m = jnp.mean(x, axis=axis, keepdims=True)
    v = jnp.var(x, axis=axis, keepdims=True)
    return (x - m) / jnp.sqrt(v + eps)

def _scatter_add(tgt, idx, src, axis=0):
    return tgt.at[idx].add(src)

def _segment_sum(src, seg, n):
    return jax.ops.segment_sum(src, seg, n)
kernel_name = 'mk_gnn_preln_d4_gnn_r32_20da6c'

def setup_inputs(seed: int=0):
    np.random.seed(seed)
    _w = jnp.asarray

    def _rec_inputs():
        import jax
        import jax.numpy as jnp
        _gk = jax.random.key(seed)
        x = -0.000202 + 1 * jax.random.normal(jax.random.fold_in(_gk, 1), (50000, 128), jnp.float32)
        src = jax.random.randint(jax.random.fold_in(_gk, 2), (50000,), 0, 50000, jnp.int32)
        dst = jnp.minimum((50000 * jax.random.uniform(jax.random.fold_in(_gk, 3), (50000,)) ** 2.0).astype(jnp.int32), 49999)
        _o = jnp.argsort(dst, stable=True)
        src = src[_o]
        dst = dst[_o]
        edge_attr_128 = 5.93493e-05 + 1.00006 * jax.random.normal(jax.random.fold_in(_gk, 13), (50000, 128), jnp.float32)
        edge_weight = 6.14103e-05 + 0.0999867 * jax.random.normal(jax.random.fold_in(_gk, 15), (50000,), jnp.float32)
        return (x, src, dst, edge_attr_128, edge_weight)
    x, src, dst, edge_attr_128, edge_weight = _rec_inputs()

    def _L0_gnn_setup():
        import jax, jax.numpy as jnp
        import numpy as np
        N = 50000
        E = 25000
        C = 128
        H = 8
        HD = C // H
        key = jax.random.key(seed)
        ks = jax.random.split(key, 8)
        s = 1.0 / np.sqrt(C)
        x = jax.random.normal(ks[0], (N, C), jnp.float32)
        edge_index = jax.random.randint(ks[1], (2, E), 0, N, jnp.int32)
        edge_weight = jax.random.normal(ks[2], (E,), jnp.float32) * 0.1
        Wq = jax.random.normal(ks[3], (C, C), jnp.float32) * s
        Wk = jax.random.normal(ks[4], (C, C), jnp.float32) * s
        Wv = jax.random.normal(ks[5], (C, C), jnp.float32) * s
        Wd = jax.random.normal(ks[6], (H, 1), jnp.float32)
        Wo = jax.random.normal(ks[7], (C, C), jnp.float32) * s
        return {'x': x, 'edge_index': edge_index, 'edge_weight': edge_weight, 'Wq': Wq, 'bq': jnp.zeros((C,), jnp.float32), 'Wk': Wk, 'bk': jnp.zeros((C,), jnp.float32), 'Wv': Wv, 'bv': jnp.zeros((C,), jnp.float32), 'Wd': Wd, 'bd': jnp.zeros((H,), jnp.float32), 'Wo': Wo, 'bo': jnp.zeros((C,), jnp.float32)}
    _L0_gnn_all = _L0_gnn_setup()
    _L0_gnn_in = {k: v for k, v in _L0_gnn_all.items() if k in ('Wq', 'bq', 'Wk', 'bk', 'Wv', 'bv', 'Wd', 'bd', 'Wo', 'bo')}
    del _L0_gnn_all

    def _L1_gnn_setup():
        import jax, jax.numpy as jnp
        import numpy as np
        N_NODES = 50000
        N_EDGES = 25000
        NUM_HEADS = 4
        HEAD_DIM = 32
        IN_DIM = 128
        NEG_SLOPE = 0.2
        key = jax.random.key(seed)
        k1, k2, k3, k4, k5, k6 = jax.random.split(key, 6)
        x = jax.random.normal(k1, (N_NODES, IN_DIM), dtype=jnp.float32)
        W = jax.random.normal(k2, (NUM_HEADS * HEAD_DIM, IN_DIM), dtype=jnp.float32) * 0.05
        attn_l = jax.random.normal(k3, (NUM_HEADS, HEAD_DIM), dtype=jnp.float32) * 0.05
        attn_r = jax.random.normal(k4, (NUM_HEADS, HEAD_DIM), dtype=jnp.float32) * 0.05
        src = jax.random.randint(k5, (N_EDGES,), 0, N_NODES, dtype=jnp.int32)
        dst = jnp.sort(jax.random.randint(k6, (N_EDGES,), 0, N_NODES, dtype=jnp.int32))
        return {'x': x, 'W': W, 'attn_l': attn_l, 'attn_r': attn_r, 'src': src, 'dst': dst}
    _L1_gnn_all = _L1_gnn_setup()
    _L1_gnn_in = {k: v for k, v in _L1_gnn_all.items() if k in ('W', 'attn_l', 'attn_r')}
    del _L1_gnn_all

    def _L2_gnn_setup():
        import jax, jax.numpy as jnp
        import numpy as np
        DIM = 128
        N_NODES = 50000
        N_EDGES = 18750
        N_GRAPHS = 128
        BN_EPS = 1e-05

        def _bn(h, gamma, beta):
            m = h.mean(axis=0)
            v = jnp.mean((h - m) ** 2, axis=0)
            return gamma * (h - m) * jax.lax.rsqrt(v + BN_EPS) + beta
        key = jax.random.key(seed)
        ks = jax.random.split(key, 16)
        x = jax.random.normal(ks[0], (N_NODES, DIM), dtype=jnp.float32)
        edge_index = jax.random.randint(ks[1], (2, N_EDGES), 0, N_NODES, dtype=jnp.int64)
        edge_attr = jax.random.normal(ks[2], (N_EDGES, DIM), dtype=jnp.float32)
        u = jax.random.normal(ks[3], (N_GRAPHS, DIM), dtype=jnp.float32)
        batch = jnp.sort(jax.random.randint(ks[4], (N_NODES,), 0, N_GRAPHS, dtype=jnp.int64))
        s0 = 1.0 / np.sqrt(3 * DIM)
        s1 = 1.0 / np.sqrt(DIM)
        W0 = jax.random.uniform(ks[5], (DIM, 3 * DIM), jnp.float32, -s0, s0)
        b0 = jax.random.uniform(ks[6], (DIM,), jnp.float32, -s0, s0)
        W1 = jax.random.uniform(ks[7], (DIM, DIM), jnp.float32, -s1, s1)
        b1 = jax.random.uniform(ks[8], (DIM,), jnp.float32, -s1, s1)
        W2 = jax.random.uniform(ks[9], (DIM, DIM), jnp.float32, -s1, s1)
        b2 = jax.random.uniform(ks[10], (DIM,), jnp.float32, -s1, s1)
        g0 = jnp.ones((DIM,), jnp.float32)
        beta0 = jnp.zeros((DIM,), jnp.float32)
        g1 = jnp.ones((DIM,), jnp.float32)
        beta1 = jnp.zeros((DIM,), jnp.float32)
        g2 = jnp.ones((DIM,), jnp.float32)
        beta2 = jnp.zeros((DIM,), jnp.float32)
        return {'x': x, 'edge_index': edge_index, 'edge_attr': edge_attr, 'u': u, 'batch': batch, 'W0': W0, 'b0': b0, 'W1': W1, 'b1': b1, 'W2': W2, 'b2': b2, 'g0': g0, 'beta0': beta0, 'g1': g1, 'beta1': beta1, 'g2': g2, 'beta2': beta2}
    _L2_gnn_all = _L2_gnn_setup()
    _L2_gnn_in = {k: v for k, v in _L2_gnn_all.items() if k in ('u', 'W0', 'b0', 'W1', 'b1', 'W2', 'b2', 'g0', 'beta0', 'g1', 'beta1', 'g2', 'beta2')}
    del _L2_gnn_all

    def _L3_gnn_setup():
        import jax, jax.numpy as jnp
        import numpy as np
        N_NODES = 50000
        N_EDGES = 20000
        IN_CH = 128
        OUT_CH = 128
        key = jax.random.key(seed)
        k1, k2, k3 = jax.random.split(key, 3)
        x = jax.random.normal(k1, (N_NODES, IN_CH), dtype=jnp.float32)
        edge_index = jax.random.randint(k2, (2, N_EDGES), 0, N_NODES, dtype=jnp.int64)
        W = jax.random.normal(k3, (OUT_CH, 2 * IN_CH), dtype=jnp.float32) * (1.0 / np.sqrt(2 * IN_CH))
        b = jnp.zeros((OUT_CH,), dtype=jnp.float32)
        return {'x': x, 'edge_index': edge_index, 'W': W, 'b': b}
    _L3_gnn_all = _L3_gnn_setup()
    _L3_gnn_in = {k: v for k, v in _L3_gnn_all.items() if k in ('W', 'b')}
    del _L3_gnn_all
    return {'x': x, 'src': src, 'dst': dst, 'edge_attr_128': edge_attr_128, 'edge_weight': edge_weight, 'L0_gnn_Wq': _L0_gnn_in['Wq'], 'L0_gnn_bq': _L0_gnn_in['bq'], 'L0_gnn_Wk': _L0_gnn_in['Wk'], 'L0_gnn_bk': _L0_gnn_in['bk'], 'L0_gnn_Wv': _L0_gnn_in['Wv'], 'L0_gnn_bv': _L0_gnn_in['bv'], 'L0_gnn_Wd': _L0_gnn_in['Wd'], 'L0_gnn_bd': _L0_gnn_in['bd'], 'L0_gnn_Wo': _L0_gnn_in['Wo'], 'L0_gnn_bo': _L0_gnn_in['bo'], 'L1_gnn_W': _L1_gnn_in['W'], 'L1_gnn_attn_l': _L1_gnn_in['attn_l'], 'L1_gnn_attn_r': _L1_gnn_in['attn_r'], 'L2_gnn_u': _L2_gnn_in['u'], 'L2_gnn_W0': _L2_gnn_in['W0'], 'L2_gnn_b0': _L2_gnn_in['b0'], 'L2_gnn_W1': _L2_gnn_in['W1'], 'L2_gnn_b1': _L2_gnn_in['b1'], 'L2_gnn_W2': _L2_gnn_in['W2'], 'L2_gnn_b2': _L2_gnn_in['b2'], 'L2_gnn_g0': _L2_gnn_in['g0'], 'L2_gnn_beta0': _L2_gnn_in['beta0'], 'L2_gnn_g1': _L2_gnn_in['g1'], 'L2_gnn_beta1': _L2_gnn_in['beta1'], 'L2_gnn_g2': _L2_gnn_in['g2'], 'L2_gnn_beta2': _L2_gnn_in['beta2'], 'L3_gnn_W': _L3_gnn_in['W'], 'L3_gnn_b': _L3_gnn_in['b']}

def reference(x, src, dst, edge_attr_128, edge_weight, L0_gnn_Wq, L0_gnn_bq, L0_gnn_Wk, L0_gnn_bk, L0_gnn_Wv, L0_gnn_bv, L0_gnn_Wd, L0_gnn_bd, L0_gnn_Wo, L0_gnn_bo, L1_gnn_W, L1_gnn_attn_l, L1_gnn_attn_r, L2_gnn_u, L2_gnn_W0, L2_gnn_b0, L2_gnn_W1, L2_gnn_b1, L2_gnn_W2, L2_gnn_b2, L2_gnn_g0, L2_gnn_beta0, L2_gnn_g1, L2_gnn_beta1, L2_gnn_g2, L2_gnn_beta2, L3_gnn_W, L3_gnn_b):
    import jax
    import jax.numpy as jnp

    def _L0_gnn_ref(x, edge_index, edge_weight, Wq, bq, Wk, bk, Wv, bv, Wd, bd, Wo, bo):
        import jax, jax.numpy as jnp
        import numpy as np
        N = 50000
        E = 25000
        C = 128
        H = 8
        HD = C // H
        row, col = (edge_index[0], edge_index[1])
        n = x.shape[0]
        q = (x @ Wq.T + bq).reshape(n, H, HD)
        k = (x @ Wk.T + bk).reshape(n, H, HD)
        v = (x @ Wv.T + bv).reshape(n, H, HD)
        scores = jnp.einsum('ehd,ehd->eh', q[row], k[col]) / np.sqrt(HD)
        scores = scores + edge_weight[:, None]
        dmean = jnp.mean(x[col] - x[row], axis=-1, keepdims=True)
        scores = scores + dmean @ Wd.T + bd
        attn = jax.nn.softmax(scores, axis=0)
        msgs = (v[col] * attn[:, :, None]).reshape(-1, H * HD)
        out = jnp.zeros((n, H * HD), x.dtype).at[row].add(msgs)
        return out @ Wo.T + bo

    def _L1_gnn_ref(x, W, attn_l, attn_r, src, dst):
        import jax, jax.numpy as jnp
        import numpy as np
        N_NODES = 50000
        N_EDGES = 25000
        NUM_HEADS = 4
        HEAD_DIM = 32
        IN_DIM = 128
        NEG_SLOPE = 0.2
        N = x.shape[0]
        H, D = attn_l.shape
        feat = (x @ W.T).reshape(N, H, D)
        el = jnp.einsum('nhd,hd->nh', feat, attn_l)
        er = jnp.einsum('nhd,hd->nh', feat, attn_r)
        e = el[src] + er[dst]
        e = jnp.where(e > 0, e, NEG_SLOPE * e)
        e_max = jax.ops.segment_max(e, dst, num_segments=N)
        e_exp = jnp.exp(e - e_max[dst])
        denom = jax.ops.segment_sum(e_exp, dst, num_segments=N)
        alpha = e_exp / denom[dst]
        out = jax.ops.segment_sum(alpha[:, :, None] * feat[src], dst, num_segments=N)
        return out.reshape(N, H * D)

    def _L2_gnn_ref(x, edge_index, edge_attr, u, batch, W0, b0, W1, b1, W2, b2, g0, beta0, g1, beta1, g2, beta2):
        import jax, jax.numpy as jnp
        import numpy as np
        DIM = 128
        N_NODES = 50000
        N_EDGES = 18750
        N_GRAPHS = 128
        BN_EPS = 1e-05

        def _bn(h, gamma, beta):
            m = h.mean(axis=0)
            v = jnp.mean((h - m) ** 2, axis=0)
            return gamma * (h - m) * jax.lax.rsqrt(v + BN_EPS) + beta
        n = x.shape[0]
        src = edge_index[0]
        sums = jax.ops.segment_sum(edge_attr, src, num_segments=n)
        cnt = jax.ops.segment_sum(jnp.ones((edge_attr.shape[0],), edge_attr.dtype), src, num_segments=n)
        v_e = sums / jnp.maximum(cnt, 1.0)[:, None]
        comb = jnp.concatenate([x, v_e, u[batch]], axis=1)
        h = _bn(jax.nn.relu(comb @ W0.T + b0), g0, beta0)
        h = _bn(jax.nn.relu(h @ W1.T + b1), g1, beta1)
        h = _bn(jax.nn.relu(h @ W2.T + b2), g2, beta2)
        return h

    def _L3_gnn_ref(x, edge_index, W, b):
        import jax, jax.numpy as jnp
        import numpy as np
        N_NODES = 50000
        N_EDGES = 20000
        IN_CH = 128
        OUT_CH = 128
        row, col = (edge_index[0], edge_index[1])
        n = x.shape[0]
        agg = jax.ops.segment_sum(x[col], row, num_segments=n)
        deg = jax.ops.segment_sum(jnp.ones((row.shape[0],), dtype=x.dtype), row, num_segments=n)
        deg = jnp.maximum(deg, 1.0)[:, None]
        agg = agg / deg
        out = jnp.concatenate([x, agg], axis=-1)
        return out @ W.T + b
    edge_index = jnp.stack([src, dst])
    batch0 = jnp.zeros((50000,), jnp.int32)
    h = jnp.maximum(_layernorm(x, axis=-1), 0.0)
    x = x + _L0_gnn_ref(h, edge_index, edge_weight, L0_gnn_Wq, L0_gnn_bq, L0_gnn_Wk, L0_gnn_bk, L0_gnn_Wv, L0_gnn_bv, L0_gnn_Wd, L0_gnn_bd, L0_gnn_Wo, L0_gnn_bo)
    h = jnp.maximum(_layernorm(x, axis=-1), 0.0)
    x = x + _L1_gnn_ref(h, L1_gnn_W, L1_gnn_attn_l, L1_gnn_attn_r, src, dst)
    h = jnp.maximum(_layernorm(x, axis=-1), 0.0)
    x = x + _L2_gnn_ref(h, edge_index, edge_attr_128, L2_gnn_u, batch0, L2_gnn_W0, L2_gnn_b0, L2_gnn_W1, L2_gnn_b1, L2_gnn_W2, L2_gnn_b2, L2_gnn_g0, L2_gnn_beta0, L2_gnn_g1, L2_gnn_beta1, L2_gnn_g2, L2_gnn_beta2)
    h = jnp.maximum(_layernorm(x, axis=-1), 0.0)
    x = x + _L3_gnn_ref(h, edge_index, L3_gnn_W, L3_gnn_b)
    return x

_drawn_inputs = setup_inputs


def setup_inputs(seed=0):
    import zlib

    import numpy as np

    out = dict(_drawn_inputs(seed))
    spreads = {'L0_gnn_bq': (0.0, 0.8),
     'L0_gnn_bk': (0.0, 0.8),
     'L0_gnn_bv': (0.0, 2.0),
     'L0_gnn_bd': (0.0, 2.0),
     'L0_gnn_bo': (0.0, 0.1),
     'L2_gnn_g0': (1.0, 0.2),
     'L2_gnn_beta0': (0.0, 0.1),
     'L2_gnn_g1': (1.0, 0.2),
     'L2_gnn_beta1': (0.0, 0.1),
     'L2_gnn_g2': (1.0, 0.2),
     'L2_gnn_beta2': (0.0, 0.1),
     'L3_gnn_b': (0.0, 0.1)}
    factors = {'edge_weight': 8.0,
     'L0_gnn_Wq': 8.0,
     'L0_gnn_Wk': 8.0,
     'L0_gnn_Wv': 8.0,
     'L0_gnn_Wd': 64.0,
     'L0_gnn_Wo': 8.0,
     'L1_gnn_attn_l': 8.0,
     'L1_gnn_attn_r': 29.363}
    for name, (base, spread) in spreads.items():
        noise = np.random.default_rng([zlib.crc32(name.encode()), seed]).standard_normal(out[name].shape)
        drawn = base * np.exp(spread * noise) if base else spread * noise
        out[name] = jnp.asarray(drawn.astype(out[name].dtype))
    for name, factor in factors.items():
        out[name] = (out[name] * factor).astype(out[name].dtype)
    return out
```

```python
from contextlib import ExitStack

import concourse.bass as bass
from concourse import mybir

ALU = mybir.AluOpType
ACT = mybir.ActivationFunctionType
AX = mybir.AxisListType
F32 = mybir.dt.float32
I32 = mybir.dt.int32
U32 = mybir.dt.uint32

P = 128
C = 128
GT = 3
REP = GT
H0, D0 = 8, 16
H1, D1 = 4, 32
MSG = 2 * C + 1
FEAT = C + H1
STATE = C + 3 * H1
LN_EPS = 1e-5
BN_EPS = 1e-5
LOW = -1e30
SLOPE = 0.2
CH = 480


class Rows:

    def __init__(self, n):
        self.n = n
        self.full = (n // P) // (2 * GT) * (2 * GT)
        self.tail = n - self.full * P
        self.loops = self.full // (2 * GT)
        self.groups = self.full // GT
        assert 0 < self.tail <= P

    def main(self, ap):
        return ap[0:self.full * P, :].rearrange("(p t) c -> p t c", p=P)

    def rest(self, ap):
        return ap[self.full * P:self.n, :]


class Group:

    def __init__(self, rows, n, h):
        self.rows, self.n, self.h = rows, n, h
        self.last = isinstance(n, int) and n == rows.loops
        self.g = n * 2 + h
        self.t0 = n * (2 * GT) + h * GT
        self.tiles = 1 if self.last else GT
        self.p = rows.tail if self.last else P

    def t(self, k):
        return self.t0 + k

    def two_before(self):
        return Group(self.rows, self.n - 1, self.h) if not (isinstance(self.n, int) and self.n == 0) else None

    def before(self):
        if self.h == 1:
            return Group(self.rows, self.n, 0)
        if isinstance(self.n, int) and self.n == 0:
            return None
        return Group(self.rows, self.n - 1, 1)


class Own:

    def __init__(self, eng, sem, per):
        self.eng, self.sem, self.per, self.k, self.base = eng, sem, per, 0, 0
        eng.sem_inc(sem, 1)

    def group(self, s):
        self.base, self.k = s.g * self.per + 1, 0
        self.eng.wait_ge(self.sem, self.base)

    def __call__(self, ins):
        ins.then_inc(self.sem, 1)
        self.k += 1

    def done(self):
        assert self.k <= self.per
        self.eng.wait_ge(self.sem, self.base + self.k)


def after(eng, sem, value):
    if not (isinstance(value, int) and value <= 0):
        eng.wait_ge(sem, value)


def hold(eng, turn, sem, value):
    if not (isinstance(value, int) and value <= 0):
        eng.wait_ge(sem, value)
        eng.sem_inc(turn, 1)


def straight(eng, rows, body):
    body(Group(rows, 0, 0))
    body(Group(rows, 0, 1))
    with eng.Fori(1, rows.loops) as i:
        body(Group(rows, i, 0))
        body(Group(rows, i, 1))
    body(Group(rows, rows.loops, 0))


def skewed(eng, rows, first, second):
    def turn(i):
        first(Group(rows, i, 1))
        second(Group(rows, i, 0))
        first(Group(rows, i + 1, 0))
        second(Group(rows, i, 1))

    first(Group(rows, 0, 0))
    turn(0)
    with eng.Fori(1, rows.loops - 1) as i:
        turn(i)
    turn(rows.loops - 1)
    second(Group(rows, rows.loops, 0))


class Kit:

    shared = []

    def __init__(self, nc, stage, ctx):
        self.nc, self.stage, self.ctx, self.taken, self.used = nc, stage, ctx, [], 0
        ctx.callback(self.clear)
        self.sp_turn, self.pool_turn, self.dve_turn = self.sem("sp_turn"), self.sem("pool_turn"), self.sem("dve_turn")

    def clear(self):
        if self.taken:
            for group in (self.taken, self.shared[0:self.used]):
                ids = [s.num for s in group]
                if ids:
                    if group is not self.taken:
                        self.nc.gpsimd.dma_reset(range(min(ids), max(ids) + 1))
                    self.nc.gpsimd.sem_clear(range(min(ids), max(ids) + 1))
            self.nc.all_engine_barrier()

    def sb(self, name, shape, dt=F32):
        return self.ctx.enter_context(self.nc.sbuf_tensor(f"{self.stage}_{name}", shape, dt))

    def ps(self, name, shape):
        return self.ctx.enter_context(self.nc.psum_tensor(f"{self.stage}_{name}", shape, F32))

    def sem(self, name):
        self.taken.append(self.ctx.enter_context(self.nc.semaphore(f"{self.stage}_{name}")))
        return self.taken[-1]

    def soft(self, n):
        got = self.shared[self.used:self.used + n]
        assert len(got) == n
        self.used += n
        return got

    def sems(self, name, n):
        return [self.sem(f"{name}{i}") for i in range(n)]

    def dram(self, name, shape, dt=F32):
        return self.nc.dram_tensor(f"{self.stage}_{name}", shape, dt).ap()


def index_columns(rows, eng, table, src, sem):
    eng.dma_start(table[:, 0:rows.full], src[0:rows.full * P].rearrange("(p t) -> p t", p=P)).then_inc(sem, 16)
    eng.dma_start(table[0:rows.tail, rows.full:rows.full + 1],
                  src[rows.full * P:rows.n].rearrange("(p o) -> p o", o=1)).then_inc(sem, 16)


def prepare(nc, w, c, scratch, rows):
    with ExitStack() as ctx:
        k = Kit(nc, "prep", ctx)
        raw = k.sb("raw", [P, 14, C])
        zeros = k.sb("zeros", [P, 1 + 3 * MSG])
        blocks = k.sb("blocks", [P, 2 * H1])
        attn = k.sb("attn", [P, 2])
        ucol = k.sb("ucol", [P, 1])
        ps = k.ps("ps", [P, 4, 512])
        loaded, made, ident_made, put = k.sem("loaded"), k.sem("made"), k.sem("ident_made"), k.sem("put")
        turned, taken, cleared, zeroed = k.sem("turned"), k.sem("taken"), k.sem("cleared"), k.sem("zeroed")
        lows = k.sb("lows", [P, STATE])
        square = [
            ("wq", w["L0_gnn_Wq"]), ("wo", w["L0_gnn_Wo"]),
            ("wk", w["L0_gnn_Wk"]), ("wv", w["L0_gnn_Wv"]),
            ("w1g", w["L1_gnn_W"]),
            ("w0a", w["L2_gnn_W0"][:, 0:C]), ("w0b", w["L2_gnn_W0"][:, C:2 * C]),
            ("w0c", w["L2_gnn_W0"][:, 2 * C:3 * C]),
            ("w1", w["L2_gnn_W1"]), ("w2", w["L2_gnn_W2"]),
            ("w3a", w["L3_gnn_W"][:, 0:C]), ("w3b", w["L3_gnn_W"][:, C:2 * C]),
        ]
        place = {
            "wq": c["wq"][:, 0:C], "wk": c["wkv"][:, 0:C], "wv": c["wkv"][:, C:2 * C], "wo": c["wo"][:, :],
            "w1g": c["wfeat"][:, 0:C], "w0a": c["w0a"][:, :], "w0b": c["w0b"][:, :], "w0c": raw[:, 12, :],
            "w1": c["w1"][:, :], "w2": c["w2"][:, :], "w3a": c["w3a"][:, :], "w3b": c["w3b"][:, :],
        }
        columns = [("b0", w["L2_gnn_b0"]), ("b1", w["L2_gnn_b1"]), ("b2", w["L2_gnn_b2"]),
                   ("g0", w["L2_gnn_g0"]), ("g1", w["L2_gnn_g1"]), ("g2", w["L2_gnn_g2"]),
                   ("t0", w["L2_gnn_beta0"]), ("t1", w["L2_gnn_beta1"]), ("t2", w["L2_gnn_beta2"])]
        rowwise = [(c["bo"][0:1, :], w["L0_gnn_bo"]), (c["b3"][0:1, :], w["L3_gnn_b"])]
        spread = [(c["bqb"][:, :], w["L0_gnn_bq"]), (c["bkvb"][:, 0:C], w["L0_gnn_bk"]),
                  (c["bkvb"][:, C:2 * C], w["L0_gnn_bv"]), (c["bd"][:, :], w["L0_gnn_bd"]),
                  (c["wdraw"][:, :], w["L0_gnn_Wd"].rearrange("h o -> (h o)"))]
        loads = len(square) + len(columns) + len(rowwise) + len(spread) + 3
        copies = 1 + 1 + len(square)
        n_sums = len(scratch["sums0"]) + len(scratch["sums3"])
        block = ctx.enter_context(nc.Block())

        @block.sync
        def _(sp):
            for i, (_, a) in enumerate(square):
                sp.dma_start(raw[:, i, :], a).then_inc(loaded, 16)
            for name, a in columns:
                sp.dma_start(c[name][:, :], a.rearrange("(p o) -> p o", o=1)).then_inc(loaded, 16)
            for to, a in rowwise:
                sp.dma_start(to, a.rearrange("(o c) -> o c", o=1)).then_inc(loaded, 16)
            for to, a in spread:
                sp.dma_start(to, a.partition_broadcast(P)).then_inc(loaded, 16)
            sp.dma_start(attn[:, 0:1], w["L1_gnn_attn_l"].rearrange("h (d o) -> (h d) o", o=1)).then_inc(loaded, 16)
            sp.dma_start(attn[:, 1:2], w["L1_gnn_attn_r"].rearrange("h (d o) -> (h d) o", o=1)).then_inc(loaded, 16)
            sp.dma_start(ucol[:, :], w["L2_gnn_u"][0:1, :].rearrange("a (p o) -> (a p) o", o=1)).then_inc(loaded, 16)
            sp.wait_ge(loaded, 16 * loads)

        @block.gpsimd
        def _(pool):
            nc.gpsimd.memset(c["ident"][:, :], 0.0)
            nc.gpsimd.memset(c["lower"][:, :], 1.0)
            nc.gpsimd.memset(c["ones"][:, :], 1.0)
            nc.gpsimd.memset(c["eps"][:, :], LN_EPS)
            nc.gpsimd.memset(zeros[:, :], 0.0)
            nc.gpsimd.iota(c["spare_i"][:, :], [[0, 1]], base=rows.n, channel_multiplier=1).then_inc(made, 1)
            pool.wait_ge(made, 1)
            nc.gpsimd.tensor_copy(c["spare"][:, :], c["spare_i"][:, :])
            nc.gpsimd.affine_select(out=c["ident"][:, :], in_=c["ident"][:, :], compare_op=ALU.not_equal,
                                    fill=1.0, base=0, pattern=[[-1, P]], channel_multiplier=1)
            nc.gpsimd.affine_select(out=c["lower"][:, :], in_=c["lower"][:, :], compare_op=ALU.is_gt,
                                    fill=0.0, base=0, pattern=[[-1, P]], channel_multiplier=1).then_inc(ident_made, 1)

        @block.tensor
        def _(pe):
            pe.wait_ge(loaded, 16 * loads)
            pe.wait_ge(ident_made, 1)
            for i in range(len(square)):
                if i >= 4:
                    pe.wait_ge(taken, i - 3)
                nc.tensor.transpose(ps[:, i % 4, 0:C], raw[:, i, :], c["ident"][:, :]).then_inc(turned, 1)
            pe.wait_ge(cleared, 2)
            pe.wait_ge(taken, len(square))
            i = [n for n, _ in square].index("w1g")
            nc.tensor.matmul(ps[:, 0, 0:2 * H1], raw[:, i, :], blocks[:, :], start=True, stop=True).then_inc(turned, 1)
            nc.tensor.matmul(ps[:, 1, 0:1], raw[:, 12, :], ucol[:, :], start=True, stop=True).then_inc(turned, 1)

        @block.vector
        def _(dve):
            nc.vector.memset(blocks[:, :], 0.0)
            nc.vector.memset(lows[:, :], 0.0).then_inc(zeroed, 1)
            dve.wait_ge(zeroed, 1)
            nc.vector.memset(lows[:, 0:H1], LOW).then_inc(zeroed, 1)
            dve.wait_ge(loaded, 16 * loads)
            for h in range(H1):
                for s in range(2):
                    nc.vector.tensor_copy(blocks[h * D1:(h + 1) * D1, s * H1 + h:s * H1 + h + 1],
                                          attn[h * D1:(h + 1) * D1, s:s + 1])
            nc.vector.tensor_scalar(c["wkv"][:, 2 * C:2 * C + H0], c["wdraw"][:, :], 1.0 / C, None, ALU.mult)
            nc.vector.tensor_scalar(c["wq"][:, C:C + H0], c["wdraw"][:, :], -1.0 / C, None,
                                    ALU.mult).then_inc(cleared, 2)
            for i, (name, _) in enumerate(square):
                dve.wait_ge(turned, i + 1)
                nc.vector.tensor_copy(place[name], ps[:, i % 4, 0:C]).then_inc(taken, 1)
            dve.wait_ge(turned, len(square) + 2)
            nc.vector.tensor_copy(c["wfeat"][:, C:C + 2 * H1], ps[:, 0, 0:2 * H1])
            nc.vector.tensor_tensor(c["b0u"][:, :], ps[:, 1, 0:1], c["b0"][:, :], ALU.add)

    return


def clear_rows(eng, rows, s, tables, zeros, width, done):
    for table in tables:
        if s.last:
            eng.dma_start(rows.rest(table), zeros[0:s.p, 0:width]).then_inc(done, 16)
            eng.dma_start(table[rows.n:rows.n + P, :], zeros[:, 0:width]).then_inc(done, 16)
        else:
            eng.dma_start(rows.main(table)[:, bass.ds(s.t0, GT), :].rearrange("p t c -> p (t c)"),
                          zeros[:, 0:GT * width]).then_inc(done, 16)


def cleared_by(rows, tables):
    return 16 * len(tables) * (rows.groups + 2)


def edge_scores(nc, w, c, scratch, rows, scores):
    with ExitStack() as ctx:
        k_ = Kit(nc, "sc", ctx)
        T1 = rows.full + 2 * GT
        ends = k_.sb("ends", [P, 2, T1], I32)
        ew = k_.sb("ew", [P, T1])
        now = k_.sb("now", [P, 2, 2, GT], I32)
        x = k_.sb("x", [P, 2, GT, 2, C])
        st = k_.sb("st", [P, 2, GT, 2, 6])
        mv = k_.sb("mv", [P, 2, GT, 2, 2])
        sd = k_.sb("sd", [P, 2, GT * 2])
        rs = k_.sb("rs", [P, 2, GT * 2])
        nb = k_.sb("nb", [P, 2, GT * 2])
        ht = k_.sb("ht", [P, 2, GT, 2, C])
        q = k_.sb("q", [P, GT, C])
        kv = k_.sb("kv", [P, 2, GT, 2 * C])
        add = k_.sb("add", [P, GT, H0])
        dot = k_.sb("dot", [P, GT, H0])
        zeros = k_.sb("zeros", [P, GT * MSG])
        ps_t = k_.ps("ps_t", [P, GT, 512])
        ps_p = k_.ps("ps_p", [P, GT, 512])
        loaded, padded = k_.sem("loaded"), k_.sem("padded")
        index_ready = k_.sem("index_ready")
        gathered = [k_.soft(GT), k_.soft(GT)]
        own_s, own_r, own_q = k_.sem("own_stats"), k_.sem("own_norm"), k_.sem("own_qk")
        stats_ready, sd_ready, norm_ready = k_.sem("stats_ready"), k_.sem("sd_ready"), k_.sem("norm_ready")
        hidden_ready, turned, turned_copied = k_.sem("hidden_ready"), k_.sem("turned"), k_.sem("turned_copied")
        projected, projected_taken = k_.sem("projected"), k_.sem("projected_taken")
        v_stored = k_.sems("v_stored", 2)
        zero_ready, cleared = k_.sem("zero_ready"), k_.sem("cleared")
        X = w["x"]
        v_main, v_tail = rows.main(scratch["v"]), rows.rest(scratch["v"])
        SLOTS = 2 * GT
        block = ctx.enter_context(nc.Block())

        @block.sync
        def _(sp):
            sp.wait_ge(padded, 3)
            index_columns(rows, sp, ends[:, 0, :], w["src"], loaded)
            index_columns(rows, sp, ends[:, 1, :], w["dst"], loaded)
            index_columns(rows, sp, ew[:, :], w["edge_weight"], loaded)

            sp.wait_ge(zero_ready, 1)

            def store(s):
                clear_rows(sp, rows, s, scratch["sums0"], zeros, MSG, cleared)
                hold(sp, k_.sp_turn, projected_taken, s.t0 + s.tiles + GT)
                if s.last:
                    sp.dma_start(v_tail, kv[0:s.p, s.h, 0, C:2 * C]).then_inc(v_stored[s.h], 16)
                else:
                    sp.dma_start(v_main[:, bass.ds(s.t0, GT), :], kv[:, s.h, :, C:2 * C]).then_inc(v_stored[s.h], 16)
            straight(sp, rows, store)
            sp.wait_ge(v_stored[0], 16 * (rows.loops + 1))
            sp.wait_ge(v_stored[1], 16 * rows.loops)
            sp.wait_ge(cleared, cleared_by(rows, scratch["sums0"]))

        @block.gpsimd
        def _(pool):
            nc.gpsimd.memset(ends[:, 0, rows.full:T1], 0)
            nc.gpsimd.memset(ends[:, 1, rows.full:T1], 0)
            nc.gpsimd.memset(ew[:, rows.full:T1], 0.0).then_inc(padded, 3)

            def gather(s):
                hold(pool, k_.pool_turn, index_ready, s.g + 1)
                for k in range(s.tiles):
                    hold(pool, k_.pool_turn, turned, s.t(k) + 1)
                    for e in range(2):
                        pool.indirect_dma_start(
                            x[0:s.p, s.h, k, e, :], None, X,
                            bass.IndirectOffsetOnAxis(ap=now[0:s.p, s.h, e, k:k + 1].bitcast(U32), axis=0),
                        ).then_inc(gathered[s.h][k], 16)
            straight(pool, rows, gather)

        @block.vector
        def _(dve):
            nc.vector.memset(zeros[:, :], 0.0).then_inc(zero_ready, 1)
            dve.wait_ge(loaded, 96)
            own1, own2, own3 = Own(dve, own_s, 1), Own(dve, own_r, 1), Own(dve, own_q, 3)

            def indices(s, t0):
                nc.vector.tensor_copy(now[:, s.h, :, :], ends[:, :, bass.ds(t0, GT)]).then_inc(index_ready, 1)

            indices(Group(rows, 0, 0), 0)
            indices(Group(rows, 0, 1), GT)

            def stats(s):
                own1.group(s)
                own2.group(s)
                for k in range(s.tiles):
                    dve.wait_ge(gathered[s.h][k], s.n * 32 + 32)
                    for e in range(2):
                        ins = nc.vector.bn_stats(st[0:s.p, s.h, k, e, :], x[0:s.p, s.h, k, e, :])
                own1(ins)
                own1.done()
                if not s.last:
                    indices(s, s.t0 + 2 * GT)
                for k in range(s.tiles):
                    for e in range(2):
                        ins = nc.vector.bn_aggr(mv[0:s.p, s.h, k, e, :], st[0:s.p, s.h, k, e, :])
                ins.then_inc(stats_ready, 1)
                dve.wait_ge(sd_ready, s.g + 1)
                m = 2 * s.tiles
                own2(nc.vector.reciprocal(rs[0:s.p, s.h, 0:m], sd[0:s.p, s.h, 0:m]))
                own2.done()
                nc.vector.scalar_tensor_tensor(
                    nb[0:s.p, s.h, 0:m], mv[0:s.p, s.h, 0:s.tiles, :, 0].rearrange("p k e -> p (k e)"), -1.0,
                    rs[0:s.p, s.h, 0:m], ALU.mult, ALU.mult).then_inc(norm_ready, 1)

            def qk(s):
                p, kk = s.p, s.tiles
                own3.group(s)
                after(dve, v_stored[s.h], s.n * 16)
                for k in range(kk):
                    dve.wait_ge(projected, s.t(k) + 1)
                    nc.vector.tensor_tensor(q[0:p, k, :], ps_p[0:p, k, 272:272 + C], c["bqb"][0:p, :], ALU.add)
                    nc.vector.tensor_scalar(add[0:p, k, :], ps_p[0:p, k, 2 * C:2 * C + H0],
                                            ew[0:p, bass.ds(s.t(k), 1)], None, ALU.add)
                    ins = nc.vector.tensor_tensor(kv[0:p, s.h, k, :], ps_p[0:p, k, 0:2 * C], c["bkvb"][0:p, :], ALU.add)
                    ins.then_inc(projected_taken, 1)
                dve.wait_ge(projected_taken, s.t0 + kk + GT)
                own3(nc.vector.tensor_tensor(q[0:p, 0:kk, :], q[0:p, 0:kk, :], kv[0:p, s.h, 0:kk, 0:C], ALU.mult))
                own3.done()
                own3(nc.vector.tensor_reduce(dot[0:p, 0:kk, :].rearrange("p k h -> p (k h)"),
                                             q[0:p, 0:kk, :].rearrange("p k (h d) -> p (k h) d", d=D0), AX.X, ALU.add))
                own3.done()
                own3(nc.vector.scalar_tensor_tensor(
                    scores[0:p, bass.ds(s.t0, kk), :].rearrange("p k h -> p (k h)"), dot[0:p, 0:kk, :].rearrange("p k h -> p (k h)"),
                    float(D0) ** -0.5, add[0:p, 0:kk, :].rearrange("p k h -> p (k h)"), ALU.mult, ALU.add))

            dve.sem_inc(projected_taken, GT)
            skewed(dve, rows, stats, qk)

        @block.scalar
        def _(act):
            def norm(s):
                p = s.p
                act.wait_ge(stats_ready, s.g + 1)
                nc.scalar.activation(sd[0:p, s.h, 0:2 * s.tiles],
                                     mv[0:p, s.h, 0:s.tiles, :, 1].rearrange("p k e -> p (k e)"),
                                     ACT.Sqrt, bias=c["eps"][0:p, :]).then_inc(sd_ready, 1)
                act.wait_ge(norm_ready, s.g + 1)
                for k in range(s.tiles):
                    for e in range(2):
                        j = 2 * k + e
                        ins = nc.scalar.activation(x[0:p, s.h, k, e, :], x[0:p, s.h, k, e, :], ACT.Relu,
                                                   bias=nb[0:p, s.h, j:j + 1], scale=rs[0:p, s.h, j:j + 1])
                    ins.then_inc(hidden_ready, 1)
                for k in range(s.tiles):
                    act.wait_ge(turned, s.t(k) + 1 + SLOTS)
                    nc.scalar.activation(ht[:, s.h, k, :, 0:p], ps_t[:, k, 0:2 * C].rearrange("q (e c) -> q e c", e=2)[:, :, 0:p],
                                         ACT.Copy).then_inc(turned_copied, 1)
            straight(act, rows, norm)

        @block.tensor
        def _(pe):
            pe.sem_inc(turned, SLOTS)
            pe.wait_ge(loaded, 96)

            def project(s):
                p = s.p
                for k in range(s.tiles):
                    pe.wait_ge(hidden_ready, s.t(k) + 1)
                    pe.wait_ge(turned_copied, s.t(k) + 1)
                    for e in range(2):
                        ins = nc.tensor.transpose(ps_t[:, k, e * C:e * C + p], x[0:p, s.h, k, e, :],
                                                  c["ident"][0:p, 0:p])
                    ins.then_inc(turned, 1)
                for k in range(s.tiles):
                    pe.wait_ge(turned_copied, s.t(k) + 1 + GT)
                    pe.wait_ge(projected_taken, s.t(k) + 1)
                    nc.tensor.matmul(ps_p[0:p, k, 0:2 * C + H0], ht[:, s.h, k, 1, 0:p], c["wkv"][:, :],
                                     start=True, stop=True)
                    nc.tensor.matmul(ps_p[0:p, k, 2 * C:2 * C + H0], ht[:, s.h, k, 0, 0:p], c["wq"][:, C:C + H0],
                                     start=False, stop=True, skip_group_check=True)
                    nc.tensor.matmul(ps_p[0:p, k, 272:272 + C], ht[:, s.h, k, 0, 0:p], c["wq"][:, 0:C],
                                     start=True, stop=True, skip_group_check=True).then_inc(projected, 1)
            pe.sem_inc(turned_copied, GT)
            straight(pe, rows, project)


def edge_weights(nc, c, rows, scores):
    with ExitStack() as ctx:
        k_ = Kit(nc, "sm", ctx)
        T = rows.full + 1
        top, tops, low = k_.sb("top", [P, H0]), k_.sb("tops", [P, H0]), k_.sb("low", [P, H0])
        part, whole, inv = k_.sb("part", [P, H0]), k_.sb("whole", [P, H0]), k_.sb("inv", [P, H0])
        own, topped, all_topped, lowered = k_.sem("own"), k_.sem("topped"), k_.sem("all_topped"), k_.sem("lowered")
        powers, summed = k_.sem("powers"), k_.sem("summed")
        by_head = scores[:, 0:T, :].rearrange("p t h -> p h t")
        block = ctx.enter_context(nc.Block())

        @block.vector
        def _(dve):
            flat = scores[:, 0:T, :]
            nc.vector.tensor_tensor(flat, flat, c["bd"][:, :].unsqueeze(1).broadcast_to([P, T, H0]), ALU.add).then_inc(own, 1)
            dve.wait_ge(own, 1)
            nc.vector.tensor_reduce(top[:, :], by_head, AX.X, ALU.max).then_inc(topped, 1)
            dve.wait_ge(all_topped, 1)
            nc.vector.tensor_scalar(low[:, :], tops[:, :], -1.0, None, ALU.mult).then_inc(lowered, 1)
            dve.wait_ge(summed, 1)
            nc.vector.reciprocal(inv[:, :], whole[:, :]).then_inc(own, 1)
            dve.wait_ge(own, 2)
            nc.vector.tensor_tensor(flat, flat, inv[:, :].unsqueeze(1).broadcast_to([P, T, H0]), ALU.mult)

        @block.gpsimd
        def _(pool):
            pool.wait_ge(topped, 1)
            nc.gpsimd.partition_all_reduce(tops[:, :], top[:, :], P, bass.bass_isa.ReduceOp.max).then_inc(all_topped, 1)
            pool.wait_ge(powers, H0)
            nc.gpsimd.partition_all_reduce(whole[:, :], part[:, :], P, bass.bass_isa.ReduceOp.add).then_inc(summed, 1)

        @block.scalar
        def _(act):
            act.wait_ge(lowered, 1)
            for h in range(H0):
                nc.scalar.activation(scores[:, 0:T, h], scores[:, 0:T, h], ACT.Exp, bias=low[:, h:h + 1],
                                     accum_out=part[:, h:h + 1]).then_inc(powers, 1)


class SameNode:

    def __init__(self, nc, k_, c, rows, nodes):
        self.nc, self.c, self.rows, self.nodes = nc, c, rows, nodes
        self.num = k_.sb("num", [P, 2, GT])
        self.same = k_.sb("same", [P, 2, GT, P])
        self.scrap = k_.sb("scrap", [P, GT, P])
        self.before = k_.sb("before", [P, 2, GT])
        self.away = k_.sb("away", [P, 2, GT])
        self.to = k_.sb("to", [P, 2, GT], I32)
        self.ps = k_.ps("ps_num", [P, 2, 512])
        self.num_ready, self.spread, self.own = k_.sem("num_ready"), k_.sem("spread"), k_.sem("own_same")

    def tensor(self, pe, s):
        p = s.p
        pe.wait_ge(self.num_ready, s.g + 1)
        for k in range(s.tiles):
            ins = self.nc.tensor.matmul(self.ps[0:p, s.h, k * P:k * P + p],
                                        self.num[0:p, s.h, k:k + 1].broadcast_to([p, p]),
                                        self.c["ident"][0:p, 0:p], start=True, stop=True)
        ins.then_inc(self.spread, 1)

    def vector_begin(self, dve, own, s):
        nc, p, kk, h = self.nc, s.p, s.tiles, s.h
        nc.vector.tensor_copy(self.num[0:p, h, 0:kk], self.nodes[0:p, bass.ds(s.t0, kk)]).then_inc(self.num_ready, 1)

    def vector(self, dve, own, s, place_free):
        nc, c, p, kk, h = self.nc, self.c, s.p, s.tiles, s.h
        num = self.num[0:p, h, 0:kk]
        dve.wait_ge(self.spread, s.g + 1)
        own(nc.vector.tensor_tensor(
            self.same[0:p, h, 0:kk, 0:p], self.ps[0:p, h, 0:kk * P].rearrange("q (k j) -> q k j", j=P)[:, :, 0:p],
            num.unsqueeze(2).broadcast_to([p, kk, p]), ALU.is_equal))
        own(nc.vector.tensor_scalar(self.away[0:p, h, 0:kk], num, -1.0, c["spare"][0:p, :], ALU.mult, ALU.add))
        own.done()
        for k in range(kk):
            ins = nc.vector.tensor_tensor_reduce(self.scrap[0:p, k, 0:p], self.same[0:p, h, k, 0:p], c["lower"][0:p, 0:p],
                                                 1.0, 0.0, ALU.mult, ALU.add, self.before[0:p, h, k:k + 1])
        own(ins)
        own.done()
        own(nc.vector.scalar_tensor_tensor(self.away[0:p, h, 0:kk], self.before[0:p, h, 0:kk], 0.0,
                                           self.away[0:p, h, 0:kk], ALU.is_gt, ALU.mult))
        place_free()
        own.done()
        own(nc.vector.tensor_tensor(self.to[0:p, h, 0:kk], self.away[0:p, h, 0:kk], num, ALU.add))


def add_by_source(nc, w, c, t, rows, scores, layer):
    first = layer == 0
    width = MSG if first else C
    tables = t["sums0"] if first else t["sums3"]
    with ExitStack() as ctx:
        k_ = Kit(nc, f"add{layer}", ctx)
        T1 = rows.full + 2 * GT
        nodes = k_.sb("nodes", [P, T1], I32)
        same = SameNode(nc, k_, c, rows, nodes)
        m = k_.sb("m", [P, 2, GT, width])
        o = k_.sb("o", [P, 2, GT, width])
        ps = k_.ps("ps_sum", [P, GT, 512])
        loaded, padded, ones_ready = k_.sem("loaded"), k_.sem("padded"), k_.sem("ones_ready")
        own_p = k_.sem("own_prepare")
        m_loaded, m_ready, summed, sum_copied = k_.sems("m_loaded", 2), k_.sem("m_ready"), k_.sem("summed"), k_.sem("sum_copied")
        added = k_.soft(REP)
        targets = None if first else k_.sb("targets", [P, T1], I32)
        now = None if first else k_.sb("now", [P, 2, GT], I32)
        now_ready, gathered = k_.sem("now_ready"), [k_.soft(GT), k_.soft(GT)]
        zeros = k_.sb("zeros", [P, GT * C]) if first else None
        zero_ready, cleared = k_.sem("zero_ready"), k_.sem("cleared")
        block = ctx.enter_context(nc.Block())
        lists = 2 if first else 4

        @block.sync
        def _(sp):
            sp.wait_ge(padded, 1)
            index_columns(rows, sp, nodes[:, :], w["src"], loaded)
            if not first:
                index_columns(rows, sp, targets[:, :], w["dst"], loaded)
                return
            sources = [(t["v"], 0), (w["edge_attr_128"], C)]

            sp.wait_ge(zero_ready, 1)

            def load(s):
                clear_rows(sp, rows, s, t["sums3"], zeros, C, cleared)
                hold(sp, k_.sp_turn, summed, s.t0 + s.tiles)
                for a, at in sources:
                    if s.last:
                        sp.dma_start(m[0:s.p, s.h, 0, at:at + C], rows.rest(a)).then_inc(m_loaded[s.h], 16)
                    else:
                        sp.dma_start(m[:, s.h, :, at:at + C],
                                     rows.main(a)[:, bass.ds(s.t0, GT), :]).then_inc(m_loaded[s.h], 16)
            straight(sp, rows, load)
            sp.wait_ge(cleared, cleared_by(rows, t["sums3"]))

        @block.gpsimd
        def _(pool):
            if not first:
                nc.gpsimd.memset(targets[:, rows.full:T1], 0)
            nc.gpsimd.memset(nodes[:, rows.full:T1], 0).then_inc(padded, 1)

            def gather(s):
                hold(pool, k_.pool_turn, now_ready, s.g + 1)
                for k in range(s.tiles):
                    hold(pool, k_.pool_turn, summed, s.t(k) + 1)
                    pool.indirect_dma_start(
                        m[0:s.p, s.h, k, :], None, t["h3"],
                        bass.IndirectOffsetOnAxis(ap=now[0:s.p, s.h, k:k + 1].bitcast(U32), axis=0),
                    ).then_inc(gathered[s.h][k], 16)

            def add(s):
                for k in range(s.tiles):
                    hold(pool, k_.pool_turn, sum_copied, s.t(k) + 1 + GT)
                    hold(pool, k_.pool_turn, added[k], s.g * 16)
                    pool.indirect_dma_start(
                        tables[k], bass.IndirectOffsetOnAxis(ap=same.to[0:s.p, s.h, k:k + 1].bitcast(U32), axis=0),
                        o[0:s.p, s.h, k, :], None, compute_op=ALU.add).then_inc(added[k], 16)

            if first:
                straight(pool, rows, add)
            else:
                skewed(pool, rows, gather, add)
            for r in range(REP):
                pool.wait_ge(added[r], 16 * (rows.groups + (1 if r == 0 else 0)))

        @block.vector
        def _(dve):
            if first:
                nc.vector.memset(m[:, :, :, 2 * C:MSG], 1.0).then_inc(ones_ready, 1)
                nc.vector.memset(zeros[:, :], 0.0).then_inc(zero_ready, 1)
            dve.wait_ge(loaded, 16 * lists)
            own = Own(dve, own_p, 5)

            def target(s):
                nc.vector.tensor_copy(now[:, s.h, :], targets[:, bass.ds(s.t0, GT)]).then_inc(now_ready, 1)

            if not first:
                target(Group(rows, 0, 0))
                target(Group(rows, 0, 1))

            def places(s):
                own.group(s)
                dve.wait_ge(summed, s.t0 + s.tiles)
                same.vector_begin(dve, own, s)

                def free():
                    for r in range(s.tiles):
                        after(dve, added[r], (s.g - 1) * 16)
                same.vector(dve, own, s, free)

            def weigh(s):
                p, kk = s.p, s.tiles
                if first:
                    dve.wait_ge(m_loaded[s.h], s.n * 32 + 32)
                    v = m[0:p, s.h, 0:kk, 0:C].rearrange("p k (h d) -> p k h d", d=D0)
                    a = scores[0:p, bass.ds(s.t0, kk), :].unsqueeze(3).broadcast_to([p, kk, H0, D0])
                    nc.vector.tensor_tensor(v, v, a, ALU.mult).then_inc(m_ready, 1)
                else:
                    for k in range(kk):
                        dve.wait_ge(gathered[s.h][k], s.n * 16 + 16)
                    if s.last:
                        return
                    nc.vector.tensor_copy(now[:, s.h, :], targets[:, bass.ds(s.t0 + 2 * GT, GT)]).then_inc(now_ready, 1)
            skewed(dve, rows, places, weigh)

        @block.scalar
        def _(act):
            act.sem_inc(sum_copied, GT)

            def copy(s):
                for k in range(s.tiles):
                    act.wait_ge(summed, s.t(k) + 1 + 2 * GT)
                    after(act, added[k], (s.g - 1) * 16)
                    nc.scalar.activation(o[0:s.p, s.h, k, :], ps[0:s.p, k, 0:width], ACT.Copy).then_inc(sum_copied, 1)
            straight(act, rows, copy)

        @block.tensor
        def _(pe):
            pe.sem_inc(summed, 2 * GT)
            if first:
                pe.wait_ge(ones_ready, 1)

            def spread(s):
                same.tensor(pe, s)

            def total(s):
                p = s.p
                pe.wait_ge(own_p, s.g * 5 + 6)
                if first:
                    pe.wait_ge(m_ready, s.g + 1)
                for k in range(s.tiles):
                    if not first:
                        pe.wait_ge(gathered[s.h][k], s.n * 16 + 16)
                    pe.wait_ge(sum_copied, s.t(k) + 1)
                    nc.tensor.matmul(ps[0:p, k, 0:width], same.same[0:p, s.h, k, 0:p], m[0:p, s.h, k, :],
                                     start=True, stop=True).then_inc(summed, 1)
            skewed(pe, rows, spread, total)


class Norm:

    def __init__(self, nc, k_, c):
        self.nc, self.c = nc, c
        self.st = k_.sb("st", [P, 2, GT, 6])
        self.mv = k_.sb("mv", [P, 2, GT, 2])
        self.sd = k_.sb("sd", [P, 2, GT])
        self.rs = k_.sb("rs", [P, 2, GT])
        self.nb = k_.sb("nb", [P, 2, GT])
        self.stats_ready, self.sd_ready, self.ready = k_.sem("stats_ready"), k_.sem("sd_ready"), k_.sem("norm_ready")
        self.turn = k_.dve_turn

    def vector(self, dve, own, s, x):
        nc, p, kk, h = self.nc, s.p, s.tiles, s.h
        for k in range(kk):
            ins = nc.vector.bn_stats(self.st[0:p, h, k, :], x[0:p, k, :])
        own(ins)
        own.done()
        dve.sem_inc(self.turn, 1)
        for k in range(kk):
            ins = nc.vector.bn_aggr(self.mv[0:p, h, k, :], self.st[0:p, h, k, :])
        ins.then_inc(self.stats_ready, 1)
        dve.wait_ge(self.sd_ready, s.g + 1)
        own(nc.vector.reciprocal(self.rs[0:p, h, 0:kk], self.sd[0:p, h, 0:kk]))
        own.done()
        nc.vector.scalar_tensor_tensor(self.nb[0:p, h, 0:kk], self.mv[0:p, h, 0:kk, 0], -1.0,
                                       self.rs[0:p, h, 0:kk], ALU.mult, ALU.mult).then_inc(self.ready, 1)

    def scalar_root(self, act, s):
        act.wait_ge(self.stats_ready, s.g + 1)
        self.nc.scalar.activation(self.sd[0:s.p, s.h, 0:s.tiles], self.mv[0:s.p, s.h, 0:s.tiles, 1], ACT.Sqrt,
                                  bias=self.c["eps"][0:s.p, :]).then_inc(self.sd_ready, 1)

    def scalar_apply(self, act, s, out, x, done):
        act.wait_ge(self.ready, s.g + 1)
        for k in range(s.tiles):
            ins = self.nc.scalar.activation(out[0:s.p, k, :], x[0:s.p, k, :], ACT.Relu,
                                            bias=self.nb[0:s.p, s.h, k:k + 1], scale=self.rs[0:s.p, s.h, k:k + 1])
        ins.then_inc(done, 1)


def load_group(eng, rows, s, to, table, at, width, sem):
    if s.last:
        eng.dma_start(to[0:s.p, 0, :], rows.rest(table)[:, at:at + width]).then_inc(sem, 16)
    else:
        eng.dma_start(to, rows.main(table)[:, bass.ds(s.t0, GT), at:at + width]).then_inc(sem, 16)


def store_group(eng, rows, s, table, of, sem):
    if s.last:
        eng.dma_start(rows.rest(table), of[0:s.p, 0, :]).then_inc(sem, 16)
    else:
        eng.dma_start(rows.main(table)[:, bass.ds(s.t0, GT), :], of).then_inc(sem, 16)


def stored(eng, rows, sems, each):
    eng.wait_ge(sems[0], 16 * each * (rows.loops + 1))
    eng.wait_ge(sems[1], 16 * each * rows.loops)


def after_attention(nc, w, c, t, rows):
    with ExitStack() as ctx:
        k_ = Kit(nc, "n1", ctx)
        norm = Norm(nc, k_, c)
        x, a = k_.sb("x", [P, 2, GT, C]), k_.sb("a", [P, 2, REP, GT, C])
        at, x1, hid = k_.sb("at", [P, 2, GT, P]), k_.sb("x1", [P, 2, GT, C]), k_.sb("hid", [P, 2, GT, C])
        hidt, feat = k_.sb("hidt", [P, 2, GT, P]), k_.sb("feat", [P, 2, GT, FEAT])
        state = k_.sb("state", [P, 2, GT, STATE])
        ps_a, ps_y, ps_h, ps_f = (k_.ps(n, [P, 512]) for n in ("ps_a", "ps_y", "ps_h", "ps_f"))
        loaded, out_done = k_.sems("loaded", 2), k_.sems("stored", 2)
        own = k_.sem("own")
        state_clear, at_ps, at_ready, y_ps = (k_.sem(n) for n in ("state_clear", "at_ps", "at_ready", "y_ps"))
        hid_ready, hidt_ps, hidt_ready, f_ps, f_ready = (k_.sem(n) for n in ("hid_ready", "hidt_ps", "hidt_ready", "f_ps", "f_ready"))
        stores = 2 + REP
        block = ctx.enter_context(nc.Block())

        @block.sync
        def _(sp):
            def load(s):
                hold(sp, k_.sp_turn, y_ps, s.g - 1)
                hold(sp, k_.sp_turn, own, 3 * (s.g - 2) + 2)
                load_group(sp, rows, s, x[:, s.h, :, :], w["x"], 0, C, loaded[s.h])
                for r in range(REP):
                    load_group(sp, rows, s, a[:, s.h, r, :, :], t["sums0"][r], 0, C, loaded[s.h])
            straight(sp, rows, load)

        @block.tensor
        def _(pe):
            def first(s):
                p = s.p
                pe.wait_ge(loaded[s.h], s.n * (16 * (1 + REP)) + 16 * (1 + REP))
                after(pe, at_ready, s.g)
                for k in range(s.tiles):
                    for r in range(REP):
                        ins = nc.tensor.matmul(ps_a[:, k * P:k * P + p], a[0:p, s.h, r, k, :], c["ident"][0:p, 0:p],
                                               start=r == 0, stop=r == REP - 1)
                ins.then_inc(at_ps, 1)
                pe.wait_ge(at_ready, s.g + 1)
                after(pe, own, 3 * (s.g - 1) + 2)
                for k in range(s.tiles):
                    nc.tensor.matmul(ps_y[0:p, k * C:(k + 1) * C], at[:, s.h, k, 0:p], c["wo"][:, :], start=True, stop=False)
                    ins = nc.tensor.matmul(ps_y[0:p, k * C:(k + 1) * C], c["ones"][0:1, 0:p], c["bo"][:, :],
                                           start=False, stop=True)
                ins.then_inc(y_ps, 1)

            def second(s):
                p = s.p
                pe.wait_ge(hid_ready, s.g + 1)
                after(pe, hidt_ready, s.g)
                for k in range(s.tiles):
                    ins = nc.tensor.transpose(ps_h[:, k * P:k * P + p], hid[0:p, s.h, k, :], c["ident"][0:p, 0:p])
                ins.then_inc(hidt_ps, 1)
                pe.wait_ge(hidt_ready, s.g + 1)
                after(pe, f_ready, s.g)
                for k in range(s.tiles):
                    ins = nc.tensor.matmul(ps_f[0:p, k * (C + 8):(k + 1) * (C + 8)], hidt[:, s.h, k, 0:p],
                                           c["wfeat"][:, :], start=True, stop=True)
                ins.then_inc(f_ps, 1)
            skewed(pe, rows, first, second)

        @block.vector
        def _(dve):
            nc.vector.memset(state[:, :, :, :], 0.0).then_inc(state_clear, 1)
            dve.wait_ge(state_clear, 1)
            nc.vector.memset(state[:, :, :, 0:H1], LOW)
            mine = Own(dve, own, 3)

            def first(s):
                p, kk = s.p, s.tiles
                mine.group(s)
                dve.wait_ge(y_ps, s.g + 1)
                after(dve, out_done[s.h], s.n * (16 * stores))
                mine(nc.vector.tensor_tensor(x1[0:p, s.h, 0:kk, :], ps_y[0:p, 0:kk * C].rearrange("p (k c) -> p k c", c=C),
                                             x[0:p, s.h, 0:kk, :], ALU.add))
                mine.done()
                norm.vector(dve, mine, s, x1[:, s.h, :, :])

            def second(s):
                p, kk = s.p, s.tiles
                dve.wait_ge(f_ps, s.g + 1)
                f = ps_f[0:p, 0:kk * (C + 8)].rearrange("p (k c) -> p k c", c=C + 8)
                nc.vector.tensor_copy(feat[0:p, s.h, 0:kk, :], f[:, :, 0:FEAT])
                nc.vector.tensor_copy(state[0:p, s.h, 0:kk, 2 * H1 + C:STATE], f[:, :, FEAT:C + 8]).then_inc(f_ready, 1)
            skewed(dve, rows, first, second)

        @block.scalar
        def _(act):
            def store(s):
                if s is None:
                    return
                act.wait_ge(f_ready, s.g + 1)
                store_group(act, rows, s, t["x1"], x1[:, s.h, :, :], out_done[s.h])
                store_group(act, rows, s, t["feat"], feat[:, s.h, :, :], out_done[s.h])
                for r in range(REP):
                    store_group(act, rows, s, t["state"][r], state[:, s.h, :, :], out_done[s.h])

            def first(s):
                store(s.two_before())
                act.wait_ge(at_ps, s.g + 1)
                nc.scalar.activation(at[:, s.h, 0:s.tiles, 0:s.p],
                                     ps_a[:, 0:s.tiles * P].rearrange("q (k p) -> q k p", p=P)[:, :, 0:s.p],
                                     ACT.Copy).then_inc(at_ready, 1)
                norm.scalar_root(act, s)

            def second(s):
                norm.scalar_apply(act, s, hid[:, s.h, :, :], x1[:, s.h, :, :], hid_ready)
                act.wait_ge(hidt_ps, s.g + 1)
                nc.scalar.activation(hidt[:, s.h, 0:s.tiles, 0:s.p],
                                     ps_h[:, 0:s.tiles * P].rearrange("q (k p) -> q k p", p=P)[:, :, 0:s.p],
                                     ACT.Copy).then_inc(hidt_ready, 1)
            skewed(act, rows, first, second)
            store(Group(rows, rows.loops, 0).before())
            store(Group(rows, rows.loops, 0))
            stored(act, rows, out_done, stores)


def add_by_target(nc, w, c, t, rows):
    with ExitStack() as ctx:
        k_ = Kit(nc, "gat", ctx)
        T1 = rows.full + 2 * GT
        ends = k_.sb("ends", [P, 2, T1], I32)
        same = SameNode(nc, k_, c, rows, ends[:, 1, :])
        now = k_.sb("now", [P, 2, 2, GT], I32)
        f = k_.sb("f", [P, 2, GT, FEAT])
        old, new = k_.sb("old", [P, 2, GT, STATE]), k_.sb("new", [P, 2, GT, STATE])
        far = k_.sb("far", [P, 2, GT, P])
        scrap = k_.sb("scrap4", [P, GT, H1, P])
        topel = k_.sb("topel", [P, 2, GT, H1])
        e = k_.sb("e", [P, 2, GT, 2 * H1])
        pw = k_.sb("pw", [P, 2, GT, 2 * H1])
        msg = k_.sb("msg", [P, 2, GT, H1 + C])
        ps_e = k_.ps("ps_e", [P, 2, 512])
        ps = k_.ps("ps_sum", [P, GT, 512])
        loaded, padded, now_ready = (k_.sem(n) for n in ("loaded", "padded", "now_ready"))
        own_p, own_t = k_.sem("own_prepare"), k_.sem("own_top")
        f_got = [k_.soft(GT), k_.soft(GT)]
        old_got, put = k_.soft(REP), k_.soft(REP)
        el_ps, el_used, tops_ready = k_.sem("el_ps"), k_.sem("el_used"), k_.sem("tops_ready")
        own_n, e_ready, pw_ready, msg_ready, summed = (
            k_.sem(n) for n in ("own_merge", "e_ready", "pw_ready", "msg_ready", "summed"))
        block = ctx.enter_context(nc.Block())

        @block.sync
        def _(sp):
            sp.wait_ge(padded, 1)
            index_columns(rows, sp, ends[:, 0, :], w["src"], loaded)
            index_columns(rows, sp, ends[:, 1, :], w["dst"], loaded)

        @block.gpsimd
        def _(pool):
            nc.gpsimd.memset(ends[:, :, rows.full:T1], 0).then_inc(padded, 1)

            def sources(s):
                hold(pool, k_.pool_turn, now_ready, s.g + 1)
                hold(pool, k_.pool_turn, msg_ready, s.g - 1)
                for k in range(s.tiles):
                    pool.indirect_dma_start(
                        f[0:s.p, s.h, k, :], None, t["feat"],
                        bass.IndirectOffsetOnAxis(ap=now[0:s.p, s.h, 0, k:k + 1].bitcast(U32), axis=0),
                    ).then_inc(f_got[s.h][k], 16)

            def states(s):
                hold(pool, k_.pool_turn, own_n, (s.g - 1) * 5 + 1)
                for k in range(s.tiles):
                    hold(pool, k_.pool_turn, put[k], s.g * 16)
                    pool.indirect_dma_start(
                        old[0:s.p, s.h, k, :], None, t["state"][k][0:rows.n, :],
                        bass.IndirectOffsetOnAxis(ap=now[0:s.p, s.h, 1, k:k + 1].bitcast(U32), axis=0),
                    ).then_inc(old_got[k], 16)

            def back(s):
                hold(pool, k_.pool_turn, own_n, s.g * 5 + 6)
                for k in range(s.tiles):
                    pool.indirect_dma_start(
                        t["state"][k], bass.IndirectOffsetOnAxis(ap=same.to[0:s.p, s.h, k:k + 1].bitcast(U32), axis=0),
                        new[0:s.p, s.h, k, :], None).then_inc(put[k], 16)

            def second(s):
                states(s)
                back(s)
            skewed(pool, rows, sources, second)
            for r in range(REP):
                pool.wait_ge(put[r], 16 * (rows.groups + (1 if r == 0 else 0)))

        @block.tensor
        def _(pe):
            def first(s):
                p = s.p
                same.tensor(pe, s)
                for k in range(s.tiles):
                    pe.wait_ge(f_got[s.h][k], s.n * 16 + 16)
                    after(pe, el_used, s.t(k) - 1)
                    for hh in range(H1):
                        ins = nc.tensor.matmul(ps_e[0:p, (s.h * GT + k) % 2, hh * P:hh * P + p],
                                               f[0:p, s.h, k, C + hh:C + hh + 1].broadcast_to([p, p]),
                                               c["ident"][0:p, 0:p], start=True, stop=True)
                    ins.then_inc(el_ps, 1)

            def second(s):
                p = s.p
                pe.wait_ge(msg_ready, s.g + 1)
                after(pe, own_n, (s.g - 1) * 5 + 6)
                for k in range(s.tiles):
                    nc.tensor.matmul(ps[0:p, k, 0:H1 + C], same.same[0:p, s.h, k, 0:p], msg[0:p, s.h, k, :],
                                     start=True, stop=True).then_inc(summed, 1)
            skewed(pe, rows, first, second)

        @block.vector
        def _(dve):
            dve.wait_ge(loaded, 64)
            own, ownt, merge = Own(dve, own_p, 5), Own(dve, own_t, 1), Own(dve, own_n, 5)

            def indices(s, t0):
                nc.vector.tensor_copy(now[:, s.h, :, :], ends[:, :, bass.ds(t0, GT)]).then_inc(now_ready, 1)
            indices(Group(rows, 0, 0), 0)
            indices(Group(rows, 0, 1), GT)

            def first(s):
                p, kk = s.p, s.tiles
                own.group(s)
                ownt.group(s)
                after(dve, summed, s.t0 - GT)
                same.vector_begin(dve, own, s)

                def free():
                    for r in range(kk):
                        after(dve, put[r], (s.g - 1) * 16)
                same.vector(dve, own, s, free)
                ownt(nc.vector.tensor_scalar(far[0:p, s.h, 0:kk, 0:p], same.same[0:p, s.h, 0:kk, 0:p], -1.0, -LOW,
                                             ALU.add, ALU.mult))
                ownt.done()
                for k in range(kk):
                    dve.wait_ge(el_ps, s.t(k) + 1)
                    dve.sem_inc(k_.dve_turn, 1)
                    for hh in range(H1):
                        ins = nc.vector.tensor_tensor_reduce(
                            scrap[0:p, k, hh, 0:p], ps_e[0:p, (s.h * GT + k) % 2, hh * P:hh * P + p], far[0:p, s.h, k, 0:p],
                            1.0, LOW, ALU.add, ALU.max, topel[0:p, s.h, k, hh:hh + 1])
                    ins.then_inc(el_used, 1)

            def second(s):
                p, kk, h = s.p, s.tiles, s.h
                merge.group(s)
                dve.wait_ge(el_used, s.t0 + kk)
                for k in range(kk):
                    dve.wait_ge(old_got[k], s.g * 16 + 16)
                o, n = old[0:p, h, 0:kk, :], new[0:p, h, 0:kk, :]
                ee, pp = e[0:p, h, 0:kk, :], pw[0:p, h, 0:kk, :]
                top_old, top_new, er = o[:, :, 0:H1], n[:, :, 0:H1], o[:, :, 2 * H1 + C:STATE]
                nc.vector.tensor_tensor(ee[:, :, 0:H1], f[0:p, h, 0:kk, C:FEAT], er, ALU.add)
                merge(nc.vector.tensor_tensor(ee[:, :, H1:2 * H1], topel[0:p, h, 0:kk, :], er, ALU.add))
                merge.done()
                flat = ee.rearrange("p k j -> p (k j)")
                merge(nc.vector.scalar_tensor_tensor(flat, flat, SLOPE, flat, ALU.mult, ALU.max))
                merge.done()
                merge(nc.vector.tensor_tensor(top_new, ee[:, :, H1:2 * H1], top_old, ALU.max))
                merge.done()
                nc.vector.tensor_tensor(pp[:, :, 0:H1], ee[:, :, 0:H1], top_new, ALU.subtract)
                nc.vector.tensor_tensor(pp[:, :, H1:2 * H1], top_old, top_new, ALU.subtract).then_inc(e_ready, 1)
                dve.wait_ge(pw_ready, s.g + 1)
                nc.vector.tensor_copy(msg[0:p, h, 0:kk, 0:H1], pp[:, :, 0:H1])
                nc.vector.tensor_tensor(
                    msg[0:p, h, 0:kk, H1:H1 + C].rearrange("p k (h d) -> p k h d", d=D1),
                    f[0:p, h, 0:kk, 0:C].rearrange("p k (h d) -> p k h d", d=D1),
                    pp[:, :, 0:H1].unsqueeze(3).broadcast_to([p, kk, H1, D1]), ALU.mult).then_inc(msg_ready, 1)
                fade = pp[:, :, H1:2 * H1]
                nc.vector.tensor_tensor(o[:, :, H1:2 * H1], o[:, :, H1:2 * H1], fade, ALU.mult)
                acc = o[:, :, 2 * H1:2 * H1 + C].rearrange("p k (h d) -> p k h d", d=D1)
                merge(nc.vector.tensor_tensor(acc, acc, fade.unsqueeze(3).broadcast_to([p, kk, H1, D1]), ALU.mult))
                nc.vector.tensor_copy(n[:, :, 2 * H1 + C:STATE], er)
                dve.wait_ge(summed, s.t0 + kk)
                merge.done()
                merge(nc.vector.tensor_tensor(n[:, :, H1:2 * H1 + C], ps[0:p, 0:kk, 0:H1 + C],
                                              o[:, :, H1:2 * H1 + C], ALU.add))
                if not s.last:
                    indices(s, s.t0 + 2 * GT)
            skewed(dve, rows, first, second)

        @block.scalar
        def _(act):
            def power(s):
                act.wait_ge(e_ready, s.g + 1)
                pp = pw[0:s.p, s.h, 0:s.tiles, :]
                nc.scalar.activation(pp, pp, ACT.Exp).then_inc(pw_ready, 1)
            straight(act, rows, power)


def columns_of(rows, s, table):
    if s.last:
        return table[:, rows.full * P:rows.n]
    return table[:, bass.ds(s.t0 * P, GT * P)]


def before_mlp(nc, w, c, t, rows):
    with ExitStack() as ctx:
        k_ = Kit(nc, "n2", ctx)
        norm = Norm(nc, k_, c)
        x1, st = k_.sb("x1", [P, 2, GT, C]), k_.sb("state", [P, 2, REP, GT, STATE])
        ea = k_.sb("ea", [P, 2, REP, GT, C + 1])
        top, wt, part, total = (k_.sb("top", [P, 2, GT, H1]), k_.sb("wt", [P, 2, REP, GT, H1]),
                                k_.sb("part", [P, 2, REP, GT, H1]), k_.sb("total", [P, 2, GT, H1]))
        acc, x2, hid = k_.sb("acc", [P, 2, GT, C]), k_.sb("x2", [P, 2, GT, C]), k_.sb("hid", [P, 2, GT, C])
        diag = k_.sb("diag", [P, 2, GT, P])
        hidt, vet, z = k_.sb("hidt", [P, 2, GT, P]), k_.sb("vet", [P, 2, GT, P]), k_.sb("z", [P, 2, GT * P])
        ps_h, ps_v, ps_z = (k_.ps(n, [P, 512]) for n in ("ps_h", "ps_v", "ps_z"))
        loaded, x2_stored, z_stored = k_.sems("loaded", 2), k_.sems("x2_stored", 2), k_.sems("z_stored", 2)
        own, diff_ready, wt_ready, hid_ready = (k_.sem(n) for n in ("own", "diff_ready", "wt_ready", "hid_ready"))
        h_ps, h_ready, v_ps, v_ready, z_ps, z_ready, z_used = (
            k_.sem(n) for n in ("h_ps", "h_ready", "v_ps", "v_ready", "z_ps", "z_ready", "z_used"))
        own_v = k_.sem("own_v")
        loads = 1 + 2 * REP
        X2_AT, STEPS = 9, 11
        block = ctx.enter_context(nc.Block())

        @block.sync
        def _(sp):
            def load(s):
                hold(sp, k_.sp_turn, own, (s.g - 1) * STEPS + 1)
                hold(sp, k_.sp_turn, v_ps, s.g - 1)
                load_group(sp, rows, s, x1[:, s.h, :, :], t["x1"], 0, C, loaded[s.h])
                for r in range(REP):
                    load_group(sp, rows, s, st[:, s.h, r, :, :], t["state"][r], 0, STATE, loaded[s.h])
                    load_group(sp, rows, s, ea[:, s.h, r, :, :], t["sums0"][r], C, C + 1, loaded[s.h])
            straight(sp, rows, load)

        @block.tensor
        def _(pe):
            def first(s):
                p = s.p
                pe.wait_ge(own_v, s.g * 5 + 6)
                after(pe, v_ready, s.g)
                for k in range(s.tiles):
                    for r in range(REP):
                        ins = nc.tensor.matmul(ps_v[:, k * P:k * P + p], ea[0:p, s.h, r, k, 0:C], diag[0:p, s.h, k, 0:p],
                                               start=r == 0, stop=r == REP - 1)
                ins.then_inc(v_ps, 1)

            def second(s):
                p, m = s.p, (s.tiles - 1) * P + s.p
                pe.wait_ge(hid_ready, s.g + 1)
                after(pe, h_ready, s.g)
                for k in range(s.tiles):
                    ins = nc.tensor.transpose(ps_h[:, k * P:k * P + p], hid[0:p, s.h, k, :], c["ident"][0:p, 0:p])
                ins.then_inc(h_ps, 1)
                pe.wait_ge(v_ready, s.g + 1)
                pe.wait_ge(h_ready, s.g + 1)
                after(pe, z_ready, s.g)
                nc.tensor.matmul(ps_z[:, 0:m], c["w0b"][:, :], vet[:, s.h, :, :].rearrange("q k p -> q (k p)")[:, 0:m],
                                 start=True, stop=False)
                nc.tensor.matmul(ps_z[:, 0:m], c["w0a"][:, :], hidt[:, s.h, :, :].rearrange("q k p -> q (k p)")[:, 0:m],
                                 start=False, stop=True).then_inc(z_ps, 1)
            skewed(pe, rows, first, second)

        @block.vector
        def _(dve):
            mine, count = Own(dve, own, STEPS), Own(dve, own_v, 5)

            def first(s):
                p, kk, h = s.p, s.tiles, s.h
                mine.group(s)
                count.group(s)
                dve.wait_ge(loaded[h], s.n * (16 * loads) + 16 * loads)
                deg = c["rdeg"][0:p, bass.ds(s.t0, kk)]
                cnt = ea[0:p, h, :, 0:kk, C]
                count(nc.vector.tensor_tensor(deg, cnt[:, 0, :], cnt[:, 1, :], ALU.add))
                count.done()
                for r in range(2, REP):
                    count(nc.vector.tensor_tensor(deg, deg, cnt[:, r, :], ALU.add))
                    count.done()
                count(nc.vector.tensor_scalar(deg, deg, 1.0, None, ALU.max))
                count.done()
                dve.sem_inc(k_.dve_turn, 1)
                count(nc.vector.reciprocal(deg, deg))
                count.done()
                after(dve, v_ps, s.g - 1)
                count(nc.vector.tensor_tensor(diag[0:p, h, 0:kk, 0:p], c["ident"][0:p, 0:p].unsqueeze(1).broadcast_to([p, kk, p]),
                                              deg.unsqueeze(2).broadcast_to([p, kk, p]), ALU.mult))
                S, tp = st[0:p, h, :, 0:kk, :], top[0:p, h, 0:kk, :]
                mine(nc.vector.tensor_tensor(tp, S[:, 0, :, 0:H1], S[:, 1, :, 0:H1], ALU.max))
                mine.done()
                for r in range(2, REP):
                    mine(nc.vector.tensor_tensor(tp, tp, S[:, r, :, 0:H1], ALU.max))
                    mine.done()
                W, Q = wt[0:p, h, :, 0:kk, :], part[0:p, h, :, 0:kk, :]
                nc.vector.tensor_tensor(W, S[:, :, :, 0:H1], tp.unsqueeze(1).broadcast_to([p, REP, kk, H1]),
                                        ALU.subtract).then_inc(diff_ready, 1)
                dve.wait_ge(wt_ready, s.g + 1)
                for r in range(REP):
                    f = S[:, r, :, 2 * H1:2 * H1 + C].rearrange("p k (h d) -> p k h d", d=D1)
                    nc.vector.tensor_tensor(f, f, W[:, r, :, :].unsqueeze(3).broadcast_to([p, kk, H1, D1]), ALU.mult)
                mine(nc.vector.tensor_tensor(Q, S[:, :, :, H1:2 * H1], W, ALU.mult))
                mine.done()
                A, L = acc[0:p, h, 0:kk, :], total[0:p, h, 0:kk, :]
                nc.vector.tensor_tensor(A, S[:, 0, :, 2 * H1:2 * H1 + C], S[:, 1, :, 2 * H1:2 * H1 + C], ALU.add)
                mine(nc.vector.tensor_tensor(L, Q[:, 0, :, :], Q[:, 1, :, :], ALU.add))
                mine.done()
                for r in range(2, REP):
                    nc.vector.tensor_tensor(A, A, S[:, r, :, 2 * H1:2 * H1 + C], ALU.add)
                    mine(nc.vector.tensor_tensor(L, L, Q[:, r, :, :], ALU.add))
                    mine.done()
                flat = L.rearrange("p k h -> p (k h)")
                mine(nc.vector.scalar_tensor_tensor(flat, flat, 0.0, flat, ALU.is_equal, ALU.add))
                mine.done()
                mine(nc.vector.reciprocal(flat, flat))
                mine.done()
                a4 = A.rearrange("p k (h d) -> p k h d", d=D1)
                mine(nc.vector.tensor_tensor(a4, a4, L.unsqueeze(3).broadcast_to([p, kk, H1, D1]), ALU.mult))
                mine.done()
                after(dve, x2_stored[h], s.n * 16)
                mine(nc.vector.tensor_tensor(x2[0:p, h, 0:kk, :], A, x1[0:p, h, 0:kk, :], ALU.add))
                mine.done()
                norm.vector(dve, mine, s, x2[:, h, :, :])

            def second(s):
                p, m = s.p, (s.tiles - 1) * P + s.p
                dve.wait_ge(z_ready, s.g + 1)
                dve.sem_inc(k_.dve_turn, 1)
                nc.vector.bn_stats(c["zstats"][:, bass.ds(s.g * 6, 6)], z[:, s.h, 0:m]).then_inc(z_used, 1)
            skewed(dve, rows, first, second)

        @block.scalar
        def _(act):
            def store(s):
                if s is None:
                    return
                act.wait_ge(own, s.g * STEPS + X2_AT + 1)
                store_group(act, rows, s, t["x2"], x2[:, s.h, :, :], x2_stored[s.h])
                act.wait_ge(z_ready, s.g + 1)
                act.dma_start(columns_of(rows, s, t["turned"]), z[:, s.h, 0:(s.tiles - 1) * P + s.p]).then_inc(z_stored[s.h], 16)

            def first(s):
                store(s.two_before())
                p, kk, h = s.p, s.tiles, s.h
                act.wait_ge(diff_ready, s.g + 1)
                W = wt[0:p, h, :, 0:kk, :].rearrange("p r k h -> p r (k h)")
                nc.scalar.activation(W, W, ACT.Exp).then_inc(wt_ready, 1)
                act.wait_ge(v_ps, s.g + 1)
                nc.scalar.activation(vet[:, h, 0:kk, 0:p], ps_v[:, 0:kk * P].rearrange("q (k p) -> q k p", p=P)[:, :, 0:p],
                                     ACT.Copy).then_inc(v_ready, 1)
                norm.scalar_root(act, s)

            def second(s):
                p, kk, h, m = s.p, s.tiles, s.h, (s.tiles - 1) * P + s.p
                norm.scalar_apply(act, s, hid[:, h, :, :], x2[:, h, :, :], hid_ready)
                act.wait_ge(h_ps, s.g + 1)
                nc.scalar.activation(hidt[:, h, 0:kk, 0:p], ps_h[:, 0:kk * P].rearrange("q (k p) -> q k p", p=P)[:, :, 0:p],
                                     ACT.Copy).then_inc(h_ready, 1)
                act.wait_ge(z_ps, s.g + 1)
                after(act, z_used, s.g - 1)
                after(act, z_stored[h], s.n * 16)
                nc.scalar.activation(z[:, h, 0:m], ps_z[:, 0:m], ACT.Relu, bias=c["b0u"][:, :]).then_inc(z_ready, 1)
            skewed(act, rows, first, second)
            store(Group(rows, rows.loops, 0).before())
            store(Group(rows, rows.loops, 0))
            stored(act, rows, x2_stored, 1)
            stored(act, rows, z_stored, 1)


def batch_norm(nc, c, rows, layer):
    gamma, beta = c[f"g{layer}"], c[f"t{layer}"]
    following = {0: ("w1", "b1"), 1: ("w2", "b2")}.get(layer)
    with ExitStack() as ctx:
        k_ = Kit(nc, f"bn{layer}", ctx)
        mv, sd, neg = k_.sb("mv", [P, 2]), k_.sb("sd", [P, 1]), k_.sb("neg", [P, 1])
        ps = k_.ps("ps", [P, 512])
        own, var_ready, sd_ready, shift_ready, product = (
            k_.sem(n) for n in ("own", "var_ready", "sd_ready", "shift_ready", "product"))
        block = ctx.enter_context(nc.Block())

        @block.vector
        def _(dve):
            nc.vector.bn_aggr(mv[:, :], c["zstats"][:, :]).then_inc(var_ready, 1)
            dve.wait_ge(sd_ready, 1)
            nc.vector.reciprocal(sd[:, :], sd[:, :]).then_inc(own, 1)
            dve.wait_ge(own, 1)
            nc.vector.tensor_tensor(c["scale"][:, :], gamma[:, :], sd[:, :], ALU.mult).then_inc(own, 1)
            dve.wait_ge(own, 2)
            nc.vector.scalar_tensor_tensor(neg[:, :], mv[:, 0:1], -1.0, c["scale"][:, :], ALU.mult, ALU.mult).then_inc(own, 1)
            dve.wait_ge(own, 3)
            nc.vector.tensor_tensor(c["shift"][:, :], neg[:, :], beta[:, :], ALU.add).then_inc(shift_ready, 1)
            if following:
                weight, bias = c[following[0]], c[following[1]]
                nc.vector.tensor_scalar(c["wnext"][:, :], weight[:, :], c["scale"][:, :], None, ALU.mult)
                dve.wait_ge(product, 1)
                nc.vector.tensor_tensor(c["bnext"][:, :], ps[:, 0:1], bias[:, :], ALU.add)

        @block.scalar
        def _(act):
            act.wait_ge(var_ready, 1)
            nc.scalar.activation(sd[:, :], mv[:, 1:2], ACT.Sqrt, bias=c["eps"][:, :]).then_inc(sd_ready, 1)

        if following:
            @block.tensor
            def _(pe):
                pe.wait_ge(shift_ready, 1)
                nc.tensor.matmul(ps[:, 0:1], c[following[0]][:, :], c["shift"][:, :], start=True, stop=True).then_inc(product, 1)


def mlp_layer(nc, c, source, target, rows, layer):
    with ExitStack() as ctx:
        k_ = Kit(nc, f"mlp{layer}", ctx)
        z, y = k_.sb("z", [P, 2, GT * P]), k_.sb("y", [P, 2, GT * P])
        ps = k_.ps("ps", [P, 2, 512])
        loaded, y_stored = k_.sems("loaded", 2), k_.sems("y_stored", 2)
        product, y_ready, counted = k_.sem("product"), k_.sem("y_ready"), k_.sem("counted")
        block = ctx.enter_context(nc.Block())

        def width(s):
            return (s.tiles - 1) * P + s.p

        @block.sync
        def _(sp):
            def load(s):
                hold(sp, k_.sp_turn, product, s.g - 1)
                sp.dma_start(z[:, s.h, 0:width(s)], columns_of(rows, s, source)).then_inc(loaded[s.h], 16)
            straight(sp, rows, load)

        @block.tensor
        def _(pe):
            def multiply(s):
                pe.wait_ge(loaded[s.h], s.n * 16 + 16)
                after(pe, y_ready, s.g - 1)
                nc.tensor.matmul(ps[:, s.h, 0:width(s)], c["wnext"][:, :], z[:, s.h, 0:width(s)],
                                 start=True, stop=True).then_inc(product, 1)
            straight(pe, rows, multiply)

        @block.scalar
        def _(act):
            def store(s):
                if s is None:
                    return
                act.wait_ge(y_ready, s.g + 1)
                act.dma_start(columns_of(rows, s, target), y[:, s.h, 0:width(s)]).then_inc(y_stored[s.h], 16)

            def relu(s):
                store(s.before())
                act.wait_ge(product, s.g + 1)
                after(act, counted, s.g - 1)
                after(act, y_stored[s.h], s.n * 16)
                nc.scalar.activation(y[:, s.h, 0:width(s)], ps[:, s.h, 0:width(s)], ACT.Relu,
                                     bias=c["bnext"][:, :]).then_inc(y_ready, 1)
            straight(act, rows, relu)
            store(Group(rows, rows.loops, 0))
            stored(act, rows, y_stored, 1)

        @block.vector
        def _(dve):
            def count(s):
                dve.wait_ge(y_ready, s.g + 1)
                dve.sem_inc(k_.dve_turn, 1)
                nc.vector.bn_stats(c["zstats"][:, bass.ds(s.g * 6, 6)], y[:, s.h, 0:width(s)]).then_inc(counted, 1)
            straight(dve, rows, count)


def after_mlp(nc, c, t, rows):
    with ExitStack() as ctx:
        k_ = Kit(nc, "n5", ctx)
        norm = Norm(nc, k_, c)
        z, y = k_.sb("z", [P, 2, GT * P]), k_.sb("y", [P, 2, GT * P])
        x2, x3, hid = k_.sb("x2", [P, 2, GT, C]), k_.sb("x3", [P, 2, GT, C]), k_.sb("hid", [P, 2, GT, C])
        ps = k_.ps("ps", [P, 2, 512])
        loaded, done = k_.sems("loaded", 2), k_.sems("stored", 2)
        own, y_ready, turned, hid_ready = (k_.sem(n) for n in ("own", "y_ready", "turned", "hid_ready"))
        block = ctx.enter_context(nc.Block())

        @block.sync
        def _(sp):
            def load(s):
                hold(sp, k_.sp_turn, own, (s.g - 2) * 3 + 2)
                hold(sp, k_.sp_turn, turned, s.g - 1)
                sp.dma_start(z[:, s.h, 0:(s.tiles - 1) * P + s.p], columns_of(rows, s, t["turned"])).then_inc(loaded[s.h], 16)
                load_group(sp, rows, s, x2[:, s.h, :, :], t["x2"], 0, C, loaded[s.h])
            straight(sp, rows, load)

        @block.scalar
        def _(act):
            def store(s):
                if s is None:
                    return
                act.wait_ge(hid_ready, s.g + 1)
                store_group(act, rows, s, t["x3"], x3[:, s.h, :, :], done[s.h])
                store_group(act, rows, s, t["h3"], hid[:, s.h, :, :], done[s.h])

            def first(s):
                store(s.two_before())
                m = (s.tiles - 1) * P + s.p
                act.wait_ge(loaded[s.h], s.n * 32 + 32)
                after(act, turned, s.g - 1)
                nc.scalar.activation(y[:, s.h, 0:m], z[:, s.h, 0:m], ACT.Identity, bias=c["shift"][:, :],
                                     scale=c["scale"][:, :]).then_inc(y_ready, 1)
                norm.scalar_root(act, s)

            def second(s):
                after(act, done[s.h], s.n * 32)
                norm.scalar_apply(act, s, hid[:, s.h, :, :], x3[:, s.h, :, :], hid_ready)
            skewed(act, rows, first, second)
            store(Group(rows, rows.loops, 0).before())
            store(Group(rows, rows.loops, 0))
            stored(act, rows, done, 2)

        @block.tensor
        def _(pe):
            def turn(s):
                pe.wait_ge(y_ready, s.g + 1)
                after(pe, own, (s.g - 2) * 3 + 2)
                for k in range(s.tiles):
                    ins = nc.tensor.transpose(ps[0:s.p, s.h, k * C:(k + 1) * C], y[:, s.h, k * P:k * P + s.p], c["ident"][:, :])
                ins.then_inc(turned, 1)
            straight(pe, rows, turn)

        @block.vector
        def _(dve):
            mine = Own(dve, own, 3)

            def add(s):
                p, kk = s.p, s.tiles
                mine.group(s)
                dve.wait_ge(turned, s.g + 1)
                dve.wait_ge(loaded[s.h], s.n * 32 + 32)
                after(dve, done[s.h], s.n * 32)
                mine(nc.vector.tensor_tensor(x3[0:p, s.h, 0:kk, :], ps[0:p, s.h, 0:kk * C].rearrange("p (k c) -> p k c", c=C),
                                             x2[0:p, s.h, 0:kk, :], ALU.add))
                mine.done()
                norm.vector(dve, mine, s, x3[:, s.h, :, :])
            straight(dve, rows, add)


def last_linear(nc, c, t, out, rows):
    with ExitStack() as ctx:
        k_ = Kit(nc, "n6", ctx)
        x3, hid = k_.sb("x3", [P, 2, GT, C]), k_.sb("hid", [P, 2, GT, C])
        a, diag = k_.sb("a", [P, 2, REP, GT, C]), k_.sb("diag", [P, 2, GT, P])
        hidt, at, y = k_.sb("hidt", [P, 2, GT, P]), k_.sb("at", [P, 2, GT, P]), k_.sb("y", [P, 2, GT, C])
        ps_h, ps_a, ps_y = (k_.ps(n, [P, 2, 512]) for n in ("ps_h", "ps_a", "ps_y"))
        loaded, done = k_.sems("loaded", 2), k_.sems("stored", 2)
        diag_ready, h_ps, a_ps, h_ready, a_ready, y_ps, y_ready = (
            k_.sem(n) for n in ("diag_ready", "h_ps", "a_ps", "h_ready", "a_ready", "y_ps", "y_ready"))
        loads = 16 * (2 + REP)
        block = ctx.enter_context(nc.Block())

        @block.sync
        def _(sp):
            def load(s):
                hold(sp, k_.sp_turn, a_ps, s.g - 1)
                hold(sp, k_.sp_turn, y_ready, s.g - 1)
                load_group(sp, rows, s, x3[:, s.h, :, :], t["x3"], 0, C, loaded[s.h])
                load_group(sp, rows, s, hid[:, s.h, :, :], t["h3"], 0, C, loaded[s.h])
                for r in range(REP):
                    load_group(sp, rows, s, a[:, s.h, r, :, :], t["sums3"][r], 0, C, loaded[s.h])
            straight(sp, rows, load)

        @block.tensor
        def _(pe):
            def first(s):
                p = s.p
                pe.wait_ge(loaded[s.h], s.n * loads + loads)
                pe.wait_ge(diag_ready, s.g + 1)
                after(pe, h_ready, s.g - 1)
                after(pe, a_ready, s.g - 1)
                for k in range(s.tiles):
                    ins = nc.tensor.transpose(ps_h[:, s.h, k * P:k * P + p], hid[0:p, s.h, k, :], c["ident"][0:p, 0:p])
                ins.then_inc(h_ps, 1)
                for k in range(s.tiles):
                    for r in range(REP):
                        ins = nc.tensor.matmul(ps_a[:, s.h, k * P:k * P + p], a[0:p, s.h, r, k, :], diag[0:p, s.h, k, 0:p],
                                               start=r == 0, stop=r == REP - 1)
                ins.then_inc(a_ps, 1)

            def second(s):
                p = s.p
                pe.wait_ge(h_ready, s.g + 1)
                pe.wait_ge(a_ready, s.g + 1)
                after(pe, y_ready, s.g - 1)
                for k in range(s.tiles):
                    to = ps_y[0:p, s.h, k * C:(k + 1) * C]
                    nc.tensor.matmul(to, hidt[:, s.h, k, 0:p], c["w3a"][:, :], start=True, stop=False)
                    nc.tensor.matmul(to, at[:, s.h, k, 0:p], c["w3b"][:, :], start=False, stop=False)
                    ins = nc.tensor.matmul(to, c["ones"][0:1, 0:p], c["b3"][:, :], start=False, stop=True)
                ins.then_inc(y_ps, 1)
            skewed(pe, rows, first, second)

        @block.scalar
        def _(act):
            def store(s):
                if s is None:
                    return
                act.wait_ge(y_ready, s.g + 1)
                store_group(act, rows, s, out, y[:, s.h, :, :], done[s.h])

            def copies(s):
                p, kk, h = s.p, s.tiles, s.h
                store(s.two_before())
                for got, src, dst, sem in ((h_ps, ps_h, hidt, h_ready), (a_ps, ps_a, at, a_ready)):
                    act.wait_ge(got, s.g + 1)
                    after(act, y_ps, s.g - 1)
                    nc.scalar.activation(dst[:, h, 0:kk, 0:p], src[:, h, 0:kk * P].rearrange("q (k p) -> q k p", p=P)[:, :, 0:p],
                                         ACT.Copy).then_inc(sem, 1)
            straight(act, rows, copies)
            last = Group(rows, rows.loops, 0)
            store(last.before())
            store(last)
            stored(act, rows, done, 1)

        @block.vector
        def _(dve):
            def first(s):
                p, kk, h = s.p, s.tiles, s.h
                after(dve, a_ps, s.g - 1)
                nc.vector.tensor_tensor(diag[0:p, h, 0:kk, 0:p], c["ident"][0:p, 0:p].unsqueeze(1).broadcast_to([p, kk, p]),
                                        c["rdeg"][0:p, bass.ds(s.t0, kk)].unsqueeze(2).broadcast_to([p, kk, p]),
                                        ALU.mult).then_inc(diag_ready, 1)

            def second(s):
                p, kk, h = s.p, s.tiles, s.h
                dve.wait_ge(y_ps, s.g + 1)
                after(dve, done[h], s.n * 16)
                dve.wait_ge(loaded[h], s.n * loads + loads)
                nc.vector.tensor_tensor(y[0:p, h, 0:kk, :], ps_y[0:p, h, 0:kk * C].rearrange("p (k c) -> p k c", c=C),
                                        x3[0:p, h, 0:kk, :], ALU.add).then_inc(y_ready, 1)
            skewed(dve, rows, first, second)


def clear_scores(nc, scores, rows):
    with ExitStack() as ctx:
        block = ctx.enter_context(nc.Block())

        @block.vector
        def _(dve):
            nc.vector.memset(scores[:, rows.full:rows.full + 1, :], LOW)


def gnn_kernel(nc, w, out):
    n = w["x"].shape[0]
    rows = Rows(n)
    T = rows.full + 1
    with ExitStack() as ctx:
        Kit.shared = [ctx.enter_context(nc.semaphore(f"soft_{i}")) for i in range(4 * GT)]
        k_ = Kit(nc, "all", ctx)
        c = {name: k_.sb(name, shape) for name, shape in {
            "ident": [P, P], "lower": [P, P], "ones": [P, P], "eps": [P, 1], "spare": [P, 1],
            "wq": [P, C + H0], "wkv": [P, 2 * C + H0], "wo": [P, C], "wfeat": [P, C + 2 * H1],
            "w0a": [P, C], "w0b": [P, C], "w1": [P, C], "w2": [P, C], "w3a": [P, C], "w3b": [P, C],
            "bo": [1, C], "b3": [1, C], "bqb": [P, C], "bkvb": [P, 2 * C], "bd": [P, H0], "wdraw": [P, H0],
            "b0": [P, 1], "b1": [P, 1], "b2": [P, 1], "g0": [P, 1], "g1": [P, 1], "g2": [P, 1],
            "t0": [P, 1], "t1": [P, 1], "t2": [P, 1], "b0u": [P, 1], "rdeg": [P, T],
            "zstats": [P, 6 * (rows.groups + 1)], "scale": [P, 1], "shift": [P, 1],
            "wnext": [P, C], "bnext": [P, 1]}.items()}
        c["spare_i"] = k_.sb("spare_i", [P, 1], I32)
        tables = {"v": k_.dram("v", [n, C]), "x1": k_.dram("x1", [n, C]), "x2": k_.dram("x2", [n, C]),
                  "x3": k_.dram("x3", [n, C]), "h3": k_.dram("h3", [n, C]), "feat": k_.dram("feat", [n, FEAT]),
                  "turned": k_.dram("turned", [C, n]), "turned2": k_.dram("turned2", [C, n]),
                  "state": [k_.dram(f"state_{r}", [n + P, STATE]) for r in range(REP)],
                  "sums0": [k_.dram(f"sums0_{r}", [n + P, MSG]) for r in range(REP)],
                  "sums3": [k_.dram(f"sums3_{r}", [n + P, C]) for r in range(REP)]}
        prepare(nc, w, c, tables, rows)
        with ExitStack() as inner:
            scores = Kit(nc, "edge", inner).sb("scores", [P, T, H0])
            clear_scores(nc, scores, rows)
            edge_scores(nc, w, c, tables, rows, scores)
            edge_weights(nc, c, rows, scores)
            add_by_source(nc, w, c, tables, rows, scores, 0)
        after_attention(nc, w, c, tables, rows)
        add_by_target(nc, w, c, tables, rows)
        before_mlp(nc, w, c, tables, rows)
        batch_norm(nc, c, rows, 0)
        mlp_layer(nc, c, tables["turned"], tables["turned2"], rows, 1)
        batch_norm(nc, c, rows, 1)
        mlp_layer(nc, c, tables["turned2"], tables["turned"], rows, 2)
        batch_norm(nc, c, rows, 2)
        after_mlp(nc, c, tables, rows)
        add_by_source(nc, w, c, tables, rows, None, 3)
        last_linear(nc, c, tables, out, rows)


_INS = ["x", "src", "dst", "edge_attr_128", "edge_weight",
        "L0_gnn_Wq", "L0_gnn_bq", "L0_gnn_Wk", "L0_gnn_bk", "L0_gnn_Wv", "L0_gnn_bv", "L0_gnn_Wd", "L0_gnn_bd",
        "L0_gnn_Wo", "L0_gnn_bo", "L1_gnn_W", "L1_gnn_attn_l", "L1_gnn_attn_r", "L2_gnn_u", "L2_gnn_W0",
        "L2_gnn_b0", "L2_gnn_W1", "L2_gnn_b1", "L2_gnn_W2", "L2_gnn_b2", "L2_gnn_g0", "L2_gnn_beta0",
        "L2_gnn_g1", "L2_gnn_beta1", "L2_gnn_g2", "L2_gnn_beta2", "L3_gnn_W", "L3_gnn_b"]


def kernel(**inputs):
    import numpy as _np
    import concourse.bacc as _bacc
    from concourse import mybir as _mybir
    from concourse.bass_utils import run_bass_kernel_spmd as _run

    nc = _bacc.Bacc("TRN2", target_bir_lowering=False, num_devices=1)
    arrays, args = {}, {}
    for name in _INS:
        a = _np.ascontiguousarray(inputs[name])
        arrays[f"in_{name}_dram"] = a
        args[name] = nc.dram_tensor(f"in_{name}_dram", a.shape, _mybir.dt.from_np(a.dtype), kind="ExternalInput").ap()
    out = nc.dram_tensor("out_0_dram", inputs["x"].shape, _mybir.dt.float32, kind="ExternalOutput").ap()
    gnn_kernel(nc, args, out)
    r = _run(nc, [arrays], core_ids=[0])
    return r.results[0]["out_0_dram"]
```

```python
from contextlib import ExitStack

import concourse.bass as bass
from concourse import mybir

ALU = mybir.AluOpType
ACT = mybir.ActivationFunctionType
AX = mybir.AxisListType
F32 = mybir.dt.float32
I32 = mybir.dt.int32
U32 = mybir.dt.uint32

P = 128
C = 128
GT = 3
REP = 2
H0, D0 = 8, 16
H1, D1 = 4, 32
MSG = 2 * C + 1
FEAT = C + H1
STATE = C + 3 * H1
LN_EPS = 1e-5
BN_EPS = 1e-5
LOW = -1e30
SLOPE = 0.2
CH = 480


class Rows:

    def __init__(self, n, turn):
        self.n, self.turn = n, turn
        self.full = n // P
        self.tail = n - self.full * P
        self.loops = self.full // (turn * GT)
        self.groups = self.full // GT
        assert 0 < self.tail < P and self.full % (turn * GT) == 0

    def main(self, ap):
        return ap[0:self.full * P, :].rearrange("(p t) c -> p t c", p=P)

    def rest(self, ap):
        return ap[self.full * P:self.n, :]


class Group:

    def __init__(self, rows, n, h):
        self.rows, self.n, self.h = rows, n, h
        self.last = isinstance(n, int) and n == rows.loops
        self.g = n * rows.turn + h
        self.t0 = n * (rows.turn * GT) + h * GT
        self.tiles = 1 if self.last else GT
        self.p = rows.tail if self.last else P
        self.width = (self.tiles - 1) * P + self.p

    def t(self, k):
        return self.t0 + k


class Own:

    def __init__(self, eng, sem, per):
        self.eng, self.sem, self.per, self.k, self.base = eng, sem, per, 0, 0
        eng.sem_inc(sem, 1)

    def group(self, s):
        self.base, self.k = s.g * self.per + 1, 0
        self.eng.wait_ge(self.sem, self.base)

    def __call__(self, ins):
        ins.then_inc(self.sem, 1)
        self.k += 1

    def done(self):
        assert self.k <= self.per
        self.eng.wait_ge(self.sem, self.base + self.k)


def after(eng, sem, value):
    if not (isinstance(value, int) and value <= 0):
        eng.wait_ge(sem, value)


def hold(eng, turn, sem, value):
    if not (isinstance(value, int) and value <= 0):
        eng.wait_ge(sem, value)
        eng.sem_inc(turn, 1)


def straight(eng, rows, body):
    body(Group(rows, 0, 0))
    body(Group(rows, 0, 1))
    with eng.Fori(1, rows.loops) as i:
        body(Group(rows, i, 0))
        body(Group(rows, i, 1))
    body(Group(rows, rows.loops, 0))


def skewed(eng, rows, first, second):
    def turn(i):
        first(Group(rows, i, 1))
        second(Group(rows, i, 0))
        first(Group(rows, i + 1, 0))
        second(Group(rows, i, 1))

    first(Group(rows, 0, 0))
    turn(0)
    with eng.Fori(1, rows.loops - 1) as i:
        turn(i)
    turn(rows.loops - 1)
    second(Group(rows, rows.loops, 0))


def pipelined(eng, rows, *phases):
    B = rows.turn
    head = 1 + max(1, *(-(-lag // B) for lag, _ in phases))

    def step(n, h):
        for lag, body in phases:
            dn, slot = divmod(h - lag, B)
            if isinstance(n, int) and not 0 <= (n + dn) * B + slot <= rows.groups:
                continue
            body(Group(rows, n + dn, slot))

    for n in range(head):
        for h in range(B):
            step(n, h)
    with eng.Fori(head, rows.loops) as i:
        for h in range(B):
            step(i, h)
    for h in range(1 + max(lag for lag, _ in phases)):
        step(rows.loops + h // B, h % B)


class Kit:

    shared = []

    def __init__(self, nc, stage, ctx):
        self.nc, self.stage, self.ctx, self.taken, self.used = nc, stage, ctx, [], 0
        ctx.callback(self.clear)
        self.sp_turn, self.pool_turn, self.dve_turn = self.sem("sp_turn"), self.sem("pool_turn"), self.sem("dve_turn")

    def clear(self):
        if self.taken:
            for group in (self.taken, self.shared[0:self.used]):
                ids = [s.num for s in group]
                if ids:
                    if group is not self.taken:
                        self.nc.gpsimd.dma_reset(range(min(ids), max(ids) + 1))
                    self.nc.gpsimd.sem_clear(range(min(ids), max(ids) + 1))
            self.nc.all_engine_barrier()

    def sb(self, name, shape, dt=F32):
        return self.ctx.enter_context(self.nc.sbuf_tensor(f"{self.stage}_{name}", shape, dt))

    def ps(self, name, shape):
        return self.ctx.enter_context(self.nc.psum_tensor(f"{self.stage}_{name}", shape, F32))

    def sem(self, name):
        self.taken.append(self.ctx.enter_context(self.nc.semaphore(f"{self.stage}_{name}")))
        return self.taken[-1]

    def soft(self, n):
        got = self.shared[self.used:self.used + n]
        assert len(got) == n
        self.used += n
        return got

    def sems(self, name, n):
        return [self.sem(f"{name}{i}") for i in range(n)]

    def dram(self, name, shape, dt=F32):
        return self.nc.dram_tensor(f"{self.stage}_{name}", shape, dt).ap()


def index_columns(rows, eng, table, src, sem):
    eng.dma_start(table[:, 0:rows.full], src[0:rows.full * P].rearrange("(p t) -> p t", p=P)).then_inc(sem, 16)
    eng.dma_start(table[0:rows.tail, rows.full:rows.full + 1],
                  src[rows.full * P:rows.n].rearrange("(p o) -> p o", o=1)).then_inc(sem, 16)


def prepare(nc, w, c, scratch, rows):
    with ExitStack() as ctx:
        k = Kit(nc, "prep", ctx)
        raw = k.sb("raw", [P, 14, C])
        zeros = k.sb("zeros", [P, 1 + 3 * MSG])
        blocks = k.sb("blocks", [P, 2 * H1])
        attn = k.sb("attn", [P, 2])
        ucol = k.sb("ucol", [P, 1])
        ps = k.ps("ps", [P, 4, 512])
        loaded, made, ident_made, put = k.sem("loaded"), k.sem("made"), k.sem("ident_made"), k.sem("put")
        turned, taken, cleared, zeroed = k.sem("turned"), k.sem("taken"), k.sem("cleared"), k.sem("zeroed")
        lows = k.sb("lows", [P, STATE])
        square = [
            ("wq", w["L0_gnn_Wq"]), ("wo", w["L0_gnn_Wo"]),
            ("wk", w["L0_gnn_Wk"]), ("wv", w["L0_gnn_Wv"]),
            ("w1g", w["L1_gnn_W"]),
            ("w0a", w["L2_gnn_W0"][:, 0:C]), ("w0b", w["L2_gnn_W0"][:, C:2 * C]),
            ("w0c", w["L2_gnn_W0"][:, 2 * C:3 * C]),
            ("w1", w["L2_gnn_W1"]), ("w2", w["L2_gnn_W2"]),
            ("w3a", w["L3_gnn_W"][:, 0:C]), ("w3b", w["L3_gnn_W"][:, C:2 * C]),
        ]
        place = {
            "wq": c["wq"][:, 0:C], "wk": c["wkv"][:, 0:C], "wv": c["wkv"][:, C:2 * C], "wo": c["wo"][:, :],
            "w1g": c["wfeat"][:, 0:C], "w0a": c["w0a"][:, :], "w0b": c["w0b"][:, :], "w0c": raw[:, 12, :],
            "w1": c["w1"][:, :], "w2": c["w2"][:, :], "w3a": c["w3a"][:, :], "w3b": c["w3b"][:, :],
        }
        columns = [("b0", w["L2_gnn_b0"]), ("b1", w["L2_gnn_b1"]), ("b2", w["L2_gnn_b2"]),
                   ("g0", w["L2_gnn_g0"]), ("g1", w["L2_gnn_g1"]), ("g2", w["L2_gnn_g2"]),
                   ("t0", w["L2_gnn_beta0"]), ("t1", w["L2_gnn_beta1"]), ("t2", w["L2_gnn_beta2"])]
        spread = [(c["bo"][:, :], w["L0_gnn_bo"]), (c["b3"][:, :], w["L3_gnn_b"]), (c["bqb"][:, :], w["L0_gnn_bq"]),
                  (c["bkvb"][:, 0:C], w["L0_gnn_bk"]),
                  (c["bkvb"][:, C:2 * C], w["L0_gnn_bv"]), (c["bd"][:, :], w["L0_gnn_bd"]),
                  (c["wdraw"][:, :], w["L0_gnn_Wd"].rearrange("h o -> (h o)"))]
        loads = len(square) + len(columns) + len(spread) + 3
        copies = 1 + 1 + len(square)
        block = ctx.enter_context(nc.Block())

        @block.sync
        def _(sp):
            for i, (_, a) in enumerate(square):
                sp.dma_start(raw[:, i, :], a).then_inc(loaded, 16)
            for name, a in columns:
                sp.dma_start(c[name][:, :], a.rearrange("(p o) -> p o", o=1)).then_inc(loaded, 16)
            for to, a in spread:
                sp.dma_start(to, a.partition_broadcast(P)).then_inc(loaded, 16)
            sp.dma_start(attn[:, 0:1], w["L1_gnn_attn_l"].rearrange("h (d o) -> (h d) o", o=1)).then_inc(loaded, 16)
            sp.dma_start(attn[:, 1:2], w["L1_gnn_attn_r"].rearrange("h (d o) -> (h d) o", o=1)).then_inc(loaded, 16)
            sp.dma_start(ucol[:, :], w["L2_gnn_u"][0:1, :].rearrange("a (p o) -> (a p) o", o=1)).then_inc(loaded, 16)
            sp.wait_ge(loaded, 16 * loads)

        @block.gpsimd
        def _(pool):
            nc.gpsimd.memset(c["ident"][:, :], 0.0)
            nc.gpsimd.memset(c["lower"][:, :], 1.0)
            nc.gpsimd.memset(c["eps"][:, :], LN_EPS)
            nc.gpsimd.memset(zeros[:, :], 0.0)
            nc.gpsimd.iota(c["spare_i"][:, :], [[P, GT]], base=rows.n, channel_multiplier=1).then_inc(made, 1)
            pool.wait_ge(made, 1)
            nc.gpsimd.tensor_copy(c["spare"][:, :], c["spare_i"][:, :])
            nc.gpsimd.affine_select(out=c["ident"][:, :], in_=c["ident"][:, :], compare_op=ALU.not_equal,
                                    fill=1.0, base=0, pattern=[[-1, P]], channel_multiplier=1)
            nc.gpsimd.affine_select(out=c["lower"][:, :], in_=c["lower"][:, :], compare_op=ALU.is_gt,
                                    fill=0.0, base=(GT - 1) * P, pattern=[[-1, GT * P]], channel_multiplier=1).then_inc(ident_made, 1)

        @block.tensor
        def _(pe):
            pe.wait_ge(loaded, 16 * loads)
            pe.wait_ge(ident_made, 1)
            for i in range(len(square)):
                if i >= 4:
                    pe.wait_ge(taken, i - 3)
                nc.tensor.transpose(ps[:, i % 4, 0:C], raw[:, i, :], c["ident"][:, :]).then_inc(turned, 1)
            pe.wait_ge(cleared, 2)
            pe.wait_ge(taken, len(square))
            i = [n for n, _ in square].index("w1g")
            nc.tensor.matmul(ps[:, 0, 0:2 * H1], raw[:, i, :], blocks[:, :], start=True, stop=True).then_inc(turned, 1)
            nc.tensor.matmul(ps[:, 1, 0:1], raw[:, 12, :], ucol[:, :], start=True, stop=True).then_inc(turned, 1)

        @block.vector
        def _(dve):
            nc.vector.memset(blocks[:, :], 0.0)
            nc.vector.memset(lows[:, :], 0.0).then_inc(zeroed, 1)
            dve.wait_ge(zeroed, 1)
            nc.vector.memset(lows[:, 0:H1], LOW).then_inc(zeroed, 1)
            dve.wait_ge(loaded, 16 * loads)
            for h in range(H1):
                for s in range(2):
                    nc.vector.tensor_copy(blocks[h * D1:(h + 1) * D1, s * H1 + h:s * H1 + h + 1],
                                          attn[h * D1:(h + 1) * D1, s:s + 1])
            nc.vector.tensor_scalar(c["wkv"][:, 2 * C:2 * C + H0], c["wdraw"][:, :], 1.0 / C, None, ALU.mult)
            nc.vector.tensor_scalar(c["wq"][:, C:C + H0], c["wdraw"][:, :], -1.0 / C, None,
                                    ALU.mult).then_inc(cleared, 2)
            for i, (name, _) in enumerate(square):
                dve.wait_ge(turned, i + 1)
                nc.vector.tensor_copy(place[name], ps[:, i % 4, 0:C]).then_inc(taken, 1)
            dve.wait_ge(turned, len(square) + 2)
            nc.vector.tensor_copy(c["wfeat"][:, C:C + 2 * H1], ps[:, 0, 0:2 * H1])
            nc.vector.tensor_tensor(c["b0u"][:, :], ps[:, 1, 0:1], c["b0"][:, :], ALU.add)


def clear_rows(eng, rows, s, table, zeros, width, done):
    if s.last:
        eng.dma_start(rows.rest(table), zeros[0:s.p, 0:width]).then_inc(done, 16)
        eng.dma_start(table[rows.n:rows.n + GT * P, :].rearrange("(p t) c -> p (t c)", p=P),
                      zeros[:, 0:GT * width]).then_inc(done, 16)
    else:
        eng.dma_start(rows.main(table)[:, bass.ds(s.t0, GT), :].rearrange("p t c -> p (t c)"),
                      zeros[:, 0:GT * width]).then_inc(done, 16)


def cleared_by(rows):
    return 16 * (rows.groups + 2)


def edge_scores(nc, w, c, scratch, rows, scores):
    with ExitStack() as ctx:
        k_ = Kit(nc, "sc", ctx)
        T1 = rows.full + 2 * GT
        ends = k_.sb("ends", [P, 2, T1], I32)
        ew = k_.sb("ew", [P, T1])
        now = k_.sb("now", [P, 2, 2, GT], I32)
        x = k_.sb("x", [P, 2, GT, 2, C])
        st = k_.sb("st", [P, 2, GT, 2, 6])
        mv = k_.sb("mv", [P, 2, GT, 2, 2])
        sd = k_.sb("sd", [P, 2, GT * 2])
        rs = k_.sb("rs", [P, 2, GT * 2])
        nb = k_.sb("nb", [P, 2, GT * 2])
        ht = k_.sb("ht", [P, 2, GT, 2, C])
        q = k_.sb("q", [P, GT, C])
        kv = k_.sb("kv", [P, 2, GT, 2 * C])
        add = k_.sb("add", [P, GT, H0])
        dot = k_.sb("dot", [P, GT, H0])
        zeros = k_.sb("zeros", [P, GT * MSG])
        ps_t = k_.ps("ps_t", [P, GT, 512])
        ps_p = k_.ps("ps_p", [P, GT, 512])
        loaded, padded = k_.sem("loaded"), k_.sem("padded")
        index_ready = k_.sem("index_ready")
        gathered = [k_.soft(GT), k_.soft(GT)]
        own_s, own_r, own_q = k_.sem("own_stats"), k_.sem("own_norm"), k_.sem("own_qk")
        stats_ready, sd_ready, norm_ready = k_.sem("stats_ready"), k_.sem("sd_ready"), k_.sem("norm_ready")
        hidden_ready, turned, turned_copied = k_.sem("hidden_ready"), k_.sem("turned"), k_.sem("turned_copied")
        projected, projected_taken = k_.sem("projected"), k_.sem("projected_taken")
        v_stored = k_.sems("v_stored", 2)
        zero_ready, cleared = k_.sem("zero_ready"), k_.sem("cleared")
        X = w["x"]
        v_main, v_tail = rows.main(scratch["v"]), rows.rest(scratch["v"])
        SLOTS = 2 * GT
        block = ctx.enter_context(nc.Block())

        @block.sync
        def _(sp):
            sp.wait_ge(padded, 3)
            index_columns(rows, sp, ends[:, 0, :], w["src"], loaded)
            index_columns(rows, sp, ends[:, 1, :], w["dst"], loaded)
            index_columns(rows, sp, ew[:, :], w["edge_weight"], loaded)

            sp.wait_ge(zero_ready, 1)

            def store(s):
                clear_rows(sp, rows, s, scratch["sums0"], zeros, MSG, cleared)
                hold(sp, k_.sp_turn, projected_taken, s.t0 + s.tiles + GT)
                if s.last:
                    sp.dma_start(v_tail, kv[0:s.p, s.h, 0, C:2 * C]).then_inc(v_stored[s.h], 16)
                else:
                    sp.dma_start(v_main[:, bass.ds(s.t0, GT), :], kv[:, s.h, :, C:2 * C]).then_inc(v_stored[s.h], 16)
            straight(sp, rows, store)
            sp.wait_ge(v_stored[0], 16 * (rows.loops + 1))
            sp.wait_ge(v_stored[1], 16 * rows.loops)
            sp.wait_ge(cleared, cleared_by(rows))

        @block.gpsimd
        def _(pool):
            nc.gpsimd.memset(ends[:, 0, rows.full:T1], 0)
            nc.gpsimd.memset(ends[:, 1, rows.full:T1], 0)
            nc.gpsimd.memset(ew[:, rows.full:T1], 0.0).then_inc(padded, 3)

            def gather(s):
                hold(pool, k_.pool_turn, index_ready, s.g + 1)
                for k in range(s.tiles):
                    hold(pool, k_.pool_turn, turned, s.t(k) + 1)
                    for e in range(2):
                        pool.indirect_dma_start(
                            x[0:s.p, s.h, k, e, :], None, X,
                            bass.IndirectOffsetOnAxis(ap=now[0:s.p, s.h, e, k:k + 1].bitcast(U32), axis=0),
                        ).then_inc(gathered[s.h][k], 16)
            straight(pool, rows, gather)

        @block.vector
        def _(dve):
            nc.vector.memset(zeros[:, :], 0.0).then_inc(zero_ready, 1)
            dve.wait_ge(loaded, 96)
            own1, own2, own3 = Own(dve, own_s, 1), Own(dve, own_r, 1), Own(dve, own_q, 3)

            def indices(s, t0):
                nc.vector.tensor_copy(now[:, s.h, :, :], ends[:, :, bass.ds(t0, GT)]).then_inc(index_ready, 1)

            indices(Group(rows, 0, 0), 0)
            indices(Group(rows, 0, 1), GT)

            def stats(s):
                own1.group(s)
                own2.group(s)
                for k in range(s.tiles):
                    dve.wait_ge(gathered[s.h][k], s.n * 32 + 32)
                    for e in range(2):
                        ins = nc.vector.bn_stats(st[0:s.p, s.h, k, e, :], x[0:s.p, s.h, k, e, :])
                own1(ins)
                own1.done()
                if not s.last:
                    indices(s, s.t0 + 2 * GT)
                for k in range(s.tiles):
                    for e in range(2):
                        ins = nc.vector.bn_aggr(mv[0:s.p, s.h, k, e, :], st[0:s.p, s.h, k, e, :])
                ins.then_inc(stats_ready, 1)
                dve.wait_ge(sd_ready, s.g + 1)
                m = 2 * s.tiles
                own2(nc.vector.reciprocal(rs[0:s.p, s.h, 0:m], sd[0:s.p, s.h, 0:m]))
                own2.done()
                nc.vector.scalar_tensor_tensor(
                    nb[0:s.p, s.h, 0:m], mv[0:s.p, s.h, 0:s.tiles, :, 0].rearrange("p k e -> p (k e)"), -1.0,
                    rs[0:s.p, s.h, 0:m], ALU.mult, ALU.mult).then_inc(norm_ready, 1)

            def qk(s):
                p, kk = s.p, s.tiles
                own3.group(s)
                after(dve, v_stored[s.h], s.n * 16)
                for k in range(kk):
                    dve.wait_ge(projected, s.t(k) + 1)
                    nc.vector.tensor_tensor(q[0:p, k, :], ps_p[0:p, k, 272:272 + C], c["bqb"][0:p, :], ALU.add)
                    nc.vector.tensor_scalar(add[0:p, k, :], ps_p[0:p, k, 2 * C:2 * C + H0],
                                            ew[0:p, bass.ds(s.t(k), 1)], None, ALU.add)
                    ins = nc.vector.tensor_tensor(kv[0:p, s.h, k, :], ps_p[0:p, k, 0:2 * C], c["bkvb"][0:p, :], ALU.add)
                    ins.then_inc(projected_taken, 1)
                dve.wait_ge(projected_taken, s.t0 + kk + GT)
                own3(nc.vector.tensor_tensor(q[0:p, 0:kk, :], q[0:p, 0:kk, :], kv[0:p, s.h, 0:kk, 0:C], ALU.mult))
                own3.done()
                own3(nc.vector.tensor_reduce(dot[0:p, 0:kk, :].rearrange("p k h -> p (k h)"),
                                             q[0:p, 0:kk, :].rearrange("p k (h d) -> p (k h) d", d=D0), AX.X, ALU.add))
                own3.done()
                own3(nc.vector.scalar_tensor_tensor(
                    scores[0:p, bass.ds(s.t0, kk), :].rearrange("p k h -> p (k h)"), dot[0:p, 0:kk, :].rearrange("p k h -> p (k h)"),
                    float(D0) ** -0.5, add[0:p, 0:kk, :].rearrange("p k h -> p (k h)"), ALU.mult, ALU.add))

            dve.sem_inc(projected_taken, GT)
            skewed(dve, rows, stats, qk)

        @block.scalar
        def _(act):
            def norm(s):
                p = s.p
                act.wait_ge(stats_ready, s.g + 1)
                nc.scalar.activation(sd[0:p, s.h, 0:2 * s.tiles],
                                     mv[0:p, s.h, 0:s.tiles, :, 1].rearrange("p k e -> p (k e)"),
                                     ACT.Sqrt, bias=c["eps"][0:p, :]).then_inc(sd_ready, 1)
                act.wait_ge(norm_ready, s.g + 1)
                for k in range(s.tiles):
                    for e in range(2):
                        j = 2 * k + e
                        ins = nc.scalar.activation(x[0:p, s.h, k, e, :], x[0:p, s.h, k, e, :], ACT.Relu,
                                                   bias=nb[0:p, s.h, j:j + 1], scale=rs[0:p, s.h, j:j + 1])
                    ins.then_inc(hidden_ready, 1)
                for k in range(s.tiles):
                    act.wait_ge(turned, s.t(k) + 1 + SLOTS)
                    nc.scalar.activation(ht[:, s.h, k, :, 0:p], ps_t[:, k, 0:2 * C].rearrange("q (e c) -> q e c", e=2)[:, :, 0:p],
                                         ACT.Copy).then_inc(turned_copied, 1)
            straight(act, rows, norm)

        @block.tensor
        def _(pe):
            pe.sem_inc(turned, SLOTS)
            pe.wait_ge(loaded, 96)

            def project(s):
                p = s.p
                for k in range(s.tiles):
                    pe.wait_ge(hidden_ready, s.t(k) + 1)
                    pe.wait_ge(turned_copied, s.t(k) + 1)
                    for e in range(2):
                        ins = nc.tensor.transpose(ps_t[:, k, e * C:e * C + p], x[0:p, s.h, k, e, :],
                                                  c["ident"][0:p, 0:p])
                    ins.then_inc(turned, 1)
                for k in range(s.tiles):
                    pe.wait_ge(turned_copied, s.t(k) + 1 + GT)
                    pe.wait_ge(projected_taken, s.t(k) + 1)
                    nc.tensor.matmul(ps_p[0:p, k, 0:2 * C + H0], ht[:, s.h, k, 1, 0:p], c["wkv"][:, :],
                                     start=True, stop=True)
                    nc.tensor.matmul(ps_p[0:p, k, 2 * C:2 * C + H0], ht[:, s.h, k, 0, 0:p], c["wq"][:, C:C + H0],
                                     start=False, stop=True, skip_group_check=True)
                    nc.tensor.matmul(ps_p[0:p, k, 272:272 + C], ht[:, s.h, k, 0, 0:p], c["wq"][:, 0:C],
                                     start=True, stop=True, skip_group_check=True).then_inc(projected, 1)
            pe.sem_inc(turned_copied, GT)
            straight(pe, rows, project)


def edge_weights(nc, c, rows, scores):
    with ExitStack() as ctx:
        k_ = Kit(nc, "sm", ctx)
        T = rows.full + 1
        top, tops, low = k_.sb("top", [P, H0]), k_.sb("tops", [P, H0]), k_.sb("low", [P, H0])
        part, whole, inv = k_.sb("part", [P, H0]), k_.sb("whole", [P, H0]), k_.sb("inv", [P, H0])
        own, topped, all_topped, lowered = k_.sem("own"), k_.sem("topped"), k_.sem("all_topped"), k_.sem("lowered")
        powers, summed = k_.sem("powers"), k_.sem("summed")
        by_head = scores[:, 0:T, :].rearrange("p t h -> p h t")
        block = ctx.enter_context(nc.Block())

        @block.vector
        def _(dve):
            flat = scores[:, 0:T, :]
            nc.vector.tensor_tensor(flat, flat, c["bd"][:, :].unsqueeze(1).broadcast_to([P, T, H0]), ALU.add).then_inc(own, 1)
            dve.wait_ge(own, 1)
            nc.vector.tensor_reduce(top[:, :], by_head, AX.X, ALU.max).then_inc(topped, 1)
            dve.wait_ge(all_topped, 1)
            nc.vector.tensor_scalar(low[:, :], tops[:, :], -1.0, None, ALU.mult).then_inc(lowered, 1)
            dve.wait_ge(summed, 1)
            nc.vector.reciprocal(inv[:, :], whole[:, :]).then_inc(own, 1)
            dve.wait_ge(own, 2)
            nc.vector.tensor_tensor(flat, flat, inv[:, :].unsqueeze(1).broadcast_to([P, T, H0]), ALU.mult)

        @block.gpsimd
        def _(pool):
            pool.wait_ge(topped, 1)
            nc.gpsimd.partition_all_reduce(tops[:, :], top[:, :], P, bass.bass_isa.ReduceOp.max).then_inc(all_topped, 1)
            pool.wait_ge(powers, H0)
            nc.gpsimd.partition_all_reduce(whole[:, :], part[:, :], P, bass.bass_isa.ReduceOp.add).then_inc(summed, 1)

        @block.scalar
        def _(act):
            act.wait_ge(lowered, 1)
            for h in range(H0):
                nc.scalar.activation(scores[:, 0:T, h], scores[:, 0:T, h], ACT.Exp, bias=low[:, h:h + 1],
                                     accum_out=part[:, h:h + 1]).then_inc(powers, 1)


def landed(s):
    return (s.n * GT + s.tiles) * 16


class SameNode:

    def __init__(self, nc, k_, c, rows, nodes):
        self.nc, self.c, self.rows, self.nodes = nc, c, rows, nodes
        self.num = k_.sb("num", [P, 2, GT])
        self.same = k_.sb("same", [P, 2, GT, GT * P])
        self.scrap = k_.sb("scrap", [P, GT, GT * P])
        self.before = k_.sb("before", [P, 2, GT])
        self.away = k_.sb("away", [P, 2, GT])
        self.to = k_.sb("to", [P, 2, GT], I32)
        self.ps = k_.ps("ps_num", [P, 2, 512])
        self.num_ready, self.spread = k_.sem("num_ready"), k_.sem("spread")

    def tensor(self, pe, s):
        p = s.p
        pe.wait_ge(self.num_ready, s.g + 1)
        for k in range(s.tiles):
            ins = self.nc.tensor.matmul(self.ps[0:p, s.h, k * P:k * P + p],
                                        self.num[0:p, s.h, k:k + 1].broadcast_to([p, p]),
                                        self.c["ident"][0:p, 0:p], start=True, stop=True)
        ins.then_inc(self.spread, 1)

    def sum(self, to, s, k, m):
        for j in range(s.tiles):
            ins = self.nc.tensor.matmul(to, self.same[0:s.p, s.h, j, k * P:k * P + s.p], m[:, j, :],
                                        start=j == 0, stop=j == s.tiles - 1)
        return ins

    def vector_begin(self, s):
        nc, p, kk, h = self.nc, s.p, s.tiles, s.h
        nc.vector.tensor_copy(self.num[0:p, h, 0:kk], self.nodes[0:p, bass.ds(s.t0, kk)]).then_inc(self.num_ready, 1)

    def vector(self, dve, own, s):
        nc, c, p, kk, h, W = self.nc, self.c, s.p, s.tiles, s.h, s.width
        num = self.num[0:p, h, 0:kk]
        dve.wait_ge(self.spread, s.g + 1)
        own(nc.vector.tensor_tensor(
            self.same[0:p, h, 0:kk, 0:W], self.ps[0:p, h, 0:W].unsqueeze(1).broadcast_to([p, kk, W]),
            num.unsqueeze(2).broadcast_to([p, kk, W]), ALU.is_equal))
        own(nc.vector.tensor_tensor(self.away[0:p, h, 0:kk], c["spare"][0:p, 0:kk], num, ALU.subtract))
        own.done()
        for k in range(kk):
            L, at = k * P + p, (GT - 1 - k) * P
            ins = nc.vector.tensor_tensor_reduce(self.scrap[0:p, k, 0:L], self.same[0:p, h, k, 0:L], c["lower"][0:p, at:at + L],
                                                 1.0, 0.0, ALU.mult, ALU.add, self.before[0:p, h, k:k + 1])
        own(ins)
        own.done()
        own(nc.vector.scalar_tensor_tensor(self.away[0:p, h, 0:kk], self.before[0:p, h, 0:kk], 0.0,
                                           self.away[0:p, h, 0:kk], ALU.is_gt, ALU.mult))

    def places(self, own, s):
        p, kk, h = s.p, s.tiles, s.h
        own(self.nc.vector.tensor_tensor(self.to[0:p, h, 0:kk], self.away[0:p, h, 0:kk], self.num[0:p, h, 0:kk], ALU.add))


def add_by_source(nc, w, c, t, rows, scores, layer):
    first = layer == 0
    width = MSG if first else C
    table = t["sums0"] if first else t["sums3"]
    with ExitStack() as ctx:
        k_ = Kit(nc, f"add{layer}", ctx)
        T1 = rows.full + 2 * GT
        nodes = k_.sb("nodes", [P, T1], I32)
        same = SameNode(nc, k_, c, rows, nodes)
        m = k_.sb("m", [P, 2, GT, width])
        o = k_.sb("o", [P, 2, GT, width])
        ps = k_.ps("ps_sum", [P, GT, 512])
        loaded, padded, ones_ready = k_.sem("loaded"), k_.sem("padded"), k_.sem("ones_ready")
        own_p = k_.sem("own_prepare")
        m_loaded, m_ready, summed, sum_copied = k_.sems("m_loaded", 2), k_.sem("m_ready"), k_.sem("summed"), k_.sem("sum_copied")
        (added,) = k_.soft(1)
        targets = None if first else k_.sb("targets", [P, T1], I32)
        now = None if first else k_.sb("now", [P, 2, GT], I32)
        now_ready, gathered = k_.sem("now_ready"), k_.soft(2)
        zeros = k_.sb("zeros", [P, GT * C]) if first else None
        zero_ready, cleared = k_.sem("zero_ready"), k_.sem("cleared")
        block = ctx.enter_context(nc.Block())
        lists = 2 if first else 4

        @block.sync
        def _(sp):
            sp.wait_ge(padded, 1)
            index_columns(rows, sp, nodes[:, :], w["src"], loaded)
            if not first:
                index_columns(rows, sp, targets[:, :], w["dst"], loaded)
                return
            sources = [(t["v"], 0), (w["edge_attr_128"], C)]
            sp.wait_ge(zero_ready, 1)

            def load(s):
                clear_rows(sp, rows, s, t["sums3"], zeros, C, cleared)
                hold(sp, k_.sp_turn, summed, s.t0 + GT)
                for a, at in sources:
                    if s.last:
                        sp.dma_start(m[0:s.p, s.h, 0, at:at + C], rows.rest(a)).then_inc(m_loaded[s.h], 16)
                    else:
                        sp.dma_start(m[:, s.h, :, at:at + C],
                                     rows.main(a)[:, bass.ds(s.t0, GT), :]).then_inc(m_loaded[s.h], 16)
            straight(sp, rows, load)
            sp.wait_ge(cleared, cleared_by(rows))

        @block.gpsimd
        def _(pool):
            if not first:
                nc.gpsimd.memset(targets[:, rows.full:T1], 0)
            nc.gpsimd.memset(nodes[:, rows.full:T1], 0).then_inc(padded, 1)

            def gather(s):
                hold(pool, k_.pool_turn, now_ready, s.g + 1)
                hold(pool, k_.pool_turn, summed, s.t0 + GT)
                for k in range(s.tiles):
                    pool.indirect_dma_start(
                        m[0:s.p, s.h, k, :], None, t["h3"],
                        bass.IndirectOffsetOnAxis(ap=now[0:s.p, s.h, k:k + 1].bitcast(U32), axis=0),
                    ).then_inc(gathered[s.h], 16)

            def add(s):
                hold(pool, k_.pool_turn, added, s.g * 16 * GT)
                for k in range(s.tiles):
                    hold(pool, k_.pool_turn, sum_copied, s.t(k) + 1 + GT)
                    pool.indirect_dma_start(
                        table, bass.IndirectOffsetOnAxis(ap=same.to[0:s.p, s.h, k:k + 1].bitcast(U32), axis=0),
                        o[0:s.p, s.h, k, :], None, compute_op=ALU.add).then_inc(added, 16)

            if first:
                straight(pool, rows, add)
            else:
                skewed(pool, rows, gather, add)
            pool.wait_ge(added, 16 * (GT * rows.groups + 1))

        @block.vector
        def _(dve):
            if first:
                nc.vector.memset(m[:, :, :, 2 * C:MSG], 1.0).then_inc(ones_ready, 1)
                nc.vector.memset(zeros[:, :], 0.0).then_inc(zero_ready, 1)
            dve.wait_ge(loaded, 16 * lists)
            own = Own(dve, own_p, 5)

            def target(s):
                nc.vector.tensor_copy(now[:, s.h, :], targets[:, bass.ds(s.t0, GT)]).then_inc(now_ready, 1)

            if not first:
                target(Group(rows, 0, 0))
                target(Group(rows, 0, 1))

            def places(s):
                own.group(s)
                same.vector_begin(s)
                dve.wait_ge(summed, s.t0 + GT)
                same.vector(dve, own, s)
                after(dve, added, (s.g - 1) * 16 * GT)
                own.done()
                same.places(own, s)

            def weigh(s):
                p, kk = s.p, s.tiles
                if first:
                    dve.wait_ge(m_loaded[s.h], s.n * 32 + 32)
                    v = m[0:p, s.h, 0:kk, 0:C].rearrange("p k (h d) -> p k h d", d=D0)
                    a = scores[0:p, bass.ds(s.t0, kk), :].unsqueeze(3).broadcast_to([p, kk, H0, D0])
                    nc.vector.tensor_tensor(v, v, a, ALU.mult).then_inc(m_ready, 1)
                else:
                    dve.wait_ge(gathered[s.h], landed(s))
                    if s.last:
                        return
                    nc.vector.tensor_copy(now[:, s.h, :], targets[:, bass.ds(s.t0 + 2 * GT, GT)]).then_inc(now_ready, 1)
            if first:
                pipelined(dve, rows, (0, places), (0, weigh))
            else:
                skewed(dve, rows, places, weigh)

        @block.scalar
        def _(act):
            act.sem_inc(sum_copied, GT)

            def copy(s):
                after(act, added, (s.g - 1) * 16 * GT)
                for k in range(s.tiles):
                    act.wait_ge(summed, s.t(k) + 1 + 2 * GT)
                    nc.scalar.activation(o[0:s.p, s.h, k, :], ps[0:s.p, k, 0:width], ACT.Copy).then_inc(sum_copied, 1)
            straight(act, rows, copy)

        @block.tensor
        def _(pe):
            pe.sem_inc(summed, 2 * GT)
            if first:
                pe.wait_ge(ones_ready, 1)

            def spread(s):
                same.tensor(pe, s)

            def total(s):
                p = s.p
                pe.wait_ge(own_p, s.g * 5 + 6)
                if first:
                    pe.wait_ge(m_ready, s.g + 1)
                else:
                    pe.wait_ge(gathered[s.h], landed(s))
                for k in range(s.tiles):
                    pe.wait_ge(sum_copied, s.t(k) + 1)
                    same.sum(ps[0:p, k, 0:width], s, k, m[0:p, s.h]).then_inc(summed, 1)
            skewed(pe, rows, spread, total)


def each_head(ap):
    return ap.rearrange("p k (h d) -> p k h d", d=D1)


class Norm:

    def __init__(self, nc, k_, c, slots):
        self.nc, self.c, self.k_ = nc, c, k_
        self.st = k_.sb("st", [P, slots, GT, 6])
        self.mv = k_.sb("mv", [P, slots, GT, 2])
        self.sd = k_.sb("sd", [P, slots, GT])
        self.rs = k_.sb("rs", [P, slots, GT])
        self.nb = k_.sb("nb", [P, slots, GT])
        self.stats_ready, self.sd_ready, self.ready, self.own = (
            k_.sem(n) for n in ("stats_ready", "sd_ready", "norm_ready", "own_norm"))

    def stats(self, dve, own, s, x):
        nc, p, kk, h = self.nc, s.p, s.tiles, s.h
        for k in range(kk):
            ins = nc.vector.bn_stats(self.st[0:p, h, k, :], x[0:p, k, :])
        own(ins)
        own.done()
        dve.sem_inc(self.k_.dve_turn, 1)
        for k in range(kk):
            ins = nc.vector.bn_aggr(self.mv[0:p, h, k, :], self.st[0:p, h, k, :])
        ins.then_inc(self.stats_ready, 1)

    def root(self, act, s):
        act.wait_ge(self.stats_ready, s.g + 1)
        self.nc.scalar.activation(self.sd[0:s.p, s.h, 0:s.tiles], self.mv[0:s.p, s.h, 0:s.tiles, 1], ACT.Sqrt,
                                  bias=self.c["eps"][0:s.p, :]).then_inc(self.sd_ready, 1)

    def factors(self, dve, s):
        nc, p, kk, h = self.nc, s.p, s.tiles, s.h
        dve.wait_ge(self.sd_ready, s.g + 1)
        nc.vector.reciprocal(self.rs[0:p, h, 0:kk], self.sd[0:p, h, 0:kk]).then_inc(self.own, 1)
        dve.wait_ge(self.own, s.g + 1)
        nc.vector.scalar_tensor_tensor(self.nb[0:p, h, 0:kk], self.mv[0:p, h, 0:kk, 0], -1.0,
                                       self.rs[0:p, h, 0:kk], ALU.mult, ALU.mult).then_inc(self.ready, 1)

    def apply(self, act, s, out, x, done):
        act.wait_ge(self.ready, s.g + 1)
        for k in range(s.tiles):
            ins = self.nc.scalar.activation(out[0:s.p, k, :], x[0:s.p, k, :], ACT.Relu,
                                            bias=self.nb[0:s.p, s.h, k:k + 1], scale=self.rs[0:s.p, s.h, k:k + 1])
        ins.then_inc(done, 1)


def load_group(eng, rows, s, to, table, at, width, sem):
    if s.last:
        eng.dma_start(to[0:s.p, 0, :], rows.rest(table)[:, at:at + width]).then_inc(sem, 16)
    else:
        eng.dma_start(to, rows.main(table)[:, bass.ds(s.t0, GT), at:at + width]).then_inc(sem, 16)


def store_group(eng, rows, s, table, of, sem):
    if s.last:
        eng.dma_start(rows.rest(table), of[0:s.p, 0, :]).then_inc(sem, 16)
    else:
        eng.dma_start(rows.main(table)[:, bass.ds(s.t0, GT), :], of).then_inc(sem, 16)


def stored(eng, rows, sems, each):
    for h, sem in enumerate(sems):
        eng.wait_ge(sem, 16 * each * (rows.loops + (1 if h == 0 else 0)))


def across(ps, s):
    return ps[:, 0:s.tiles * P].rearrange("q (k p) -> q k p", p=P)[:, :, 0:s.p]


def tiles_in(ps, s, width=C):
    return ps[0:s.p, 0:s.tiles * width].rearrange("p (k c) -> p k c", c=width)


def after_attention(nc, w, c, t, rows):
    with ExitStack() as ctx:
        k_ = Kit(nc, "n1", ctx)
        B = rows.turn
        norm = Norm(nc, k_, c, B)
        x, a = k_.sb("x", [P, B, GT, C]), k_.sb("a", [P, B, GT, C])
        at, x1, hid = k_.sb("at", [P, B, GT, P]), k_.sb("x1", [P, B, GT, C]), k_.sb("hid", [P, B, GT, C])
        hidt, feat = k_.sb("hidt", [P, B, GT, P]), k_.sb("feat", [P, B, GT, FEAT])
        state = k_.sb("state", [P, B, GT, STATE])
        ps_a, ps_y, ps_h, ps_f = (k_.ps(n, [P, 512]) for n in ("ps_a", "ps_y", "ps_h", "ps_f"))
        loaded, x1_stored, out_done = k_.sems("loaded", B), k_.sems("x1_stored", B), k_.sems("stored", B)
        own, biased = k_.sem("own"), k_.sem("biased")
        state_clear, a_ps, at_ready, y_ps = (k_.sem(n) for n in ("state_clear", "a_ps", "at_ready", "y_ps"))
        hid_ready, h_ps, hidt_ready, f_ps, f_ready = (k_.sem(n) for n in ("hid_ready", "h_ps", "hidt_ready", "f_ps", "f_ready"))
        stores = 16 * (1 + REP)
        block = ctx.enter_context(nc.Block())

        @block.sync
        def _(sp):
            def load(s):
                hold(sp, k_.sp_turn, a_ps, s.g - B + 1)
                hold(sp, k_.sp_turn, own, 2 * (s.g - B) + 2)
                load_group(sp, rows, s, x[:, s.h, :, :], w["x"], 0, C, loaded[s.h])
                load_group(sp, rows, s, a[:, s.h, :, :], t["sums0"], 0, C, loaded[s.h])

            def store_x1(s):
                hold(sp, k_.sp_turn, own, s.g * 2 + 2)
                store_group(sp, rows, s, t["x1"], x1[:, s.h, :, :], x1_stored[s.h])

            def store(s):
                hold(sp, k_.sp_turn, f_ready, s.g + 1)
                store_group(sp, rows, s, t["feat"], feat[:, s.h, :, :], out_done[s.h])
                for r in range(REP):
                    store_group(sp, rows, s, t["state"][r], state[:, s.h, :, :], out_done[s.h])
            pipelined(sp, rows, (9, store), (4, store_x1), (0, load))
            stored(sp, rows, x1_stored, 1)
            stored(sp, rows, out_done, stores // 16)

        @block.gpsimd
        def _(pool):
            def bias(s):
                p, kk, h = s.p, s.tiles, s.h
                hold(pool, k_.pool_turn, loaded[h], s.n * 32 + 32)
                nc.gpsimd.tensor_tensor(x[0:p, h, 0:kk, :], x[0:p, h, 0:kk, :],
                                        c["bo"][0:p, :].unsqueeze(1).broadcast_to([p, kk, C]), ALU.add).then_inc(biased, 1)
            pipelined(pool, rows, (1, bias))

        @block.tensor
        def _(pe):
            def turn_sums(s):
                pe.wait_ge(loaded[s.h], s.n * 32 + 32)
                after(pe, at_ready, s.g)
                for k in range(s.tiles):
                    ins = nc.tensor.transpose(ps_a[:, k * P:k * P + s.p], a[0:s.p, s.h, k, :], c["ident"][0:s.p, 0:s.p])
                ins.then_inc(a_ps, 1)

            def output(s):
                pe.wait_ge(at_ready, s.g + 1)
                after(pe, own, 2 * (s.g - 1) + 2)
                for k in range(s.tiles):
                    ins = nc.tensor.matmul(ps_y[0:s.p, k * C:(k + 1) * C], at[:, s.h, k, 0:s.p], c["wo"][:, :],
                                           start=True, stop=True)
                ins.then_inc(y_ps, 1)

            def turn_hidden(s):
                pe.wait_ge(hid_ready, s.g + 1)
                after(pe, hidt_ready, s.g)
                for k in range(s.tiles):
                    ins = nc.tensor.transpose(ps_h[:, k * P:k * P + s.p], hid[0:s.p, s.h, k, :], c["ident"][0:s.p, 0:s.p])
                ins.then_inc(h_ps, 1)

            def features(s):
                pe.wait_ge(hidt_ready, s.g + 1)
                after(pe, f_ready, s.g)
                for k in range(s.tiles):
                    ins = nc.tensor.matmul(ps_f[0:s.p, k * (C + 8):(k + 1) * (C + 8)], hidt[:, s.h, k, 0:s.p],
                                           c["wfeat"][:, :], start=True, stop=True)
                ins.then_inc(f_ps, 1)
            pipelined(pe, rows, (1, output), (0, turn_sums), (6, features), (5, turn_hidden))

        @block.vector
        def _(dve):
            nc.vector.memset(state[:, :, :, :], 0.0).then_inc(state_clear, 1)
            dve.wait_ge(state_clear, 1)
            nc.vector.memset(state[:, :, :, 0:H1], LOW)
            mine = Own(dve, own, 2)

            def residual(s):
                p, kk = s.p, s.tiles
                mine.group(s)
                dve.wait_ge(y_ps, s.g + 1)
                dve.wait_ge(biased, s.g + 1)
                after(dve, x1_stored[s.h], s.n * 16)
                after(dve, hid_ready, s.g - B + 1)
                mine(nc.vector.tensor_tensor(x1[0:p, s.h, 0:kk, :], tiles_in(ps_y, s), x[0:p, s.h, 0:kk, :], ALU.add))
                mine.done()
                norm.stats(dve, mine, s, x1[:, s.h, :, :])

            def spread(s):
                p, kk = s.p, s.tiles
                dve.wait_ge(f_ps, s.g + 1)
                after(dve, out_done[s.h], s.n * stores)
                f = tiles_in(ps_f, s, C + 8)
                nc.vector.tensor_copy(feat[0:p, s.h, 0:kk, :], f[:, :, 0:FEAT])
                nc.vector.tensor_copy(state[0:p, s.h, 0:kk, 2 * H1 + C:STATE], f[:, :, FEAT:C + 8]).then_inc(f_ready, 1)
            pipelined(dve, rows, (2, residual), (7, spread), (4, lambda s: norm.factors(dve, s)))

        @block.scalar
        def _(act):
            def copy_sums(s):
                act.wait_ge(a_ps, s.g + 1)
                after(act, y_ps, s.g - B + 1)
                nc.scalar.activation(at[:, s.h, 0:s.tiles, 0:s.p], across(ps_a, s), ACT.Copy).then_inc(at_ready, 1)

            def copy_hidden(s):
                act.wait_ge(h_ps, s.g + 1)
                after(act, f_ps, s.g - B + 1)
                nc.scalar.activation(hidt[:, s.h, 0:s.tiles, 0:s.p], across(ps_h, s), ACT.Copy).then_inc(hidt_ready, 1)

            def relu(s):
                after(act, h_ps, s.g - B + 1)
                norm.apply(act, s, hid[:, s.h, :, :], x1[:, s.h, :, :], hid_ready)
            pipelined(act, rows, (1, copy_sums), (5, relu), (6, copy_hidden), (3, lambda s: norm.root(act, s)))


def tiles_of(row, s):
    return row[:, 0:s.tiles * P].rearrange("p (k j) -> p k j", j=P)[:, :, 0:s.p]


def add_by_target(nc, w, c, t, rows):
    with ExitStack() as ctx:
        k_ = Kit(nc, "gat", ctx)
        T1 = rows.full + 2 * GT
        ends = k_.sb("ends", [P, 2, T1], I32)
        same = SameNode(nc, k_, c, rows, ends[:, 1, :])
        now = k_.sb("now", [P, 2, 2, GT], I32)
        f = k_.sb("f", [P, 2, GT, FEAT])
        old, new = k_.sb("old", [P, 2, GT, STATE]), k_.sb("new", [P, 2, GT, STATE])
        far = k_.sb("far", [P, 2, GT, GT * P])
        scrap = k_.sb("scrap4", [P, GT, H1, GT * P])
        topel = k_.sb("topel", [P, 2, GT, H1])
        e = k_.sb("e", [P, 2, GT, 2 * H1])
        pw = k_.sb("pw", [P, 2, GT, 2 * H1])
        msg = k_.sb("msg", [P, 2, GT, H1 + C])
        ps_e = k_.ps("ps_e", [P, GT, 512])
        ps = k_.ps("ps_sum", [P, GT, 512])
        loaded, padded, now_ready = (k_.sem(n) for n in ("loaded", "padded", "now_ready"))
        own_p, far_ready = k_.sem("own_prepare"), k_.sem("far_ready")
        f_got, old_got, put = (k_.soft(2) for _ in range(3))
        el_ps, el_used, tops_ready = k_.sem("el_ps"), k_.sem("el_used"), k_.sem("tops_ready")
        own_n, e_ready, pw_ready, msg_ready, summed = (
            k_.sem(n) for n in ("own_merge", "e_ready", "pw_ready", "msg_ready", "summed"))
        block = ctx.enter_context(nc.Block())

        @block.sync
        def _(sp):
            sp.wait_ge(padded, 1)
            index_columns(rows, sp, ends[:, 0, :], w["src"], loaded)
            index_columns(rows, sp, ends[:, 1, :], w["dst"], loaded)

        @block.gpsimd
        def _(pool):
            nc.gpsimd.memset(ends[:, :, rows.full:T1], 0).then_inc(padded, 1)

            def sources(s):
                hold(pool, k_.pool_turn, now_ready, s.g + 1)
                hold(pool, k_.pool_turn, msg_ready, s.g - 1)
                for k in range(s.tiles):
                    pool.indirect_dma_start(
                        f[0:s.p, s.h, k, :], None, t["feat"],
                        bass.IndirectOffsetOnAxis(ap=now[0:s.p, s.h, 0, k:k + 1].bitcast(U32), axis=0),
                    ).then_inc(f_got[s.h], 16)

            def states(s):
                hold(pool, k_.pool_turn, own_n, (s.g - 1) * 6 + 1)
                hold(pool, k_.pool_turn, put[s.h], s.n * 16 * GT)
                for k in range(s.tiles):
                    pool.indirect_dma_start(
                        old[0:s.p, s.h, k, :], None, t["state"][s.h][0:rows.n, :],
                        bass.IndirectOffsetOnAxis(ap=now[0:s.p, s.h, 1, k:k + 1].bitcast(U32), axis=0),
                    ).then_inc(old_got[s.h], 16)

            def back(s):
                hold(pool, k_.pool_turn, own_n, s.g * 6 + 7)
                for k in range(s.tiles):
                    pool.indirect_dma_start(
                        t["state"][s.h], bass.IndirectOffsetOnAxis(ap=same.to[0:s.p, s.h, k:k + 1].bitcast(U32), axis=0),
                        new[0:s.p, s.h, k, :], None).then_inc(put[s.h], 16)

            pipelined(pool, rows, (0, sources), (1, states), (2, back))
            pool.wait_ge(put[0], 16 * (GT * rows.loops + 1))
            pool.wait_ge(put[1], 16 * GT * rows.loops)

        @block.tensor
        def _(pe):
            def source_scores(s):
                p = s.p
                after(pe, el_used, s.t0)
                pe.wait_ge(f_got[s.h], landed(s))
                for k in range(s.tiles):
                    for hh in range(H1):
                        ins = nc.tensor.matmul(ps_e[0:p, k, hh * P:hh * P + p],
                                               f[0:p, s.h, k, C + hh:C + hh + 1].broadcast_to([p, p]),
                                               c["ident"][0:p, 0:p], start=True, stop=True)
                ins.then_inc(el_ps, 1)

            def sums(s):
                p = s.p
                pe.wait_ge(msg_ready, s.g + 1)
                after(pe, own_n, (s.g - 1) * 6 + 7)
                for k in range(s.tiles):
                    same.sum(ps[0:p, k, 0:H1 + C], s, k, msg[0:p, s.h]).then_inc(summed, 1)
            pipelined(pe, rows, (1, source_scores), (0, lambda s: same.tensor(pe, s)), (2, sums))

        @block.vector
        def _(dve):
            dve.wait_ge(loaded, 64)
            own, merge = Own(dve, own_p, 4), Own(dve, own_n, 6)

            def indices(s, t0):
                nc.vector.tensor_copy(now[:, s.h, :, :], ends[:, :, bass.ds(t0, GT)]).then_inc(now_ready, 1)
            indices(Group(rows, 0, 0), 0)
            indices(Group(rows, 0, 1), GT)

            def equals(s):
                own.group(s)
                after(dve, summed, s.t0 - GT)
                same.vector(dve, own, s)

            def tops(s):
                p, kk = s.p, s.tiles
                dve.wait_ge(far_ready, s.g + 1)
                dve.wait_ge(el_ps, s.g + 1)
                after(dve, el_used, s.t0)
                dve.sem_inc(k_.dve_turn, 1)
                for k in range(kk):
                    for hh in range(H1):
                        ins = nc.vector.tensor_tensor_reduce(
                            tiles_of(scrap[0:p, k, hh, :], s), ps_e[0:p, 0:kk, hh * P:hh * P + p], tiles_of(far[0:p, s.h, k, :], s),
                            1.0, LOW, ALU.add, ALU.max, topel[0:p, s.h, k, hh:hh + 1])
                    ins.then_inc(el_used, 1)

            def powers(s):
                p, kk, h = s.p, s.tiles, s.h
                merge.group(s)
                dve.wait_ge(el_used, s.t0 + kk)
                dve.wait_ge(old_got[s.h], landed(s))
                dve.wait_ge(f_got[s.h], landed(s))
                dve.wait_ge(own_p, s.g * 4 + 5)
                after(dve, put[s.h], s.n * 16 * GT)
                same.places(merge, s)
                if not s.last:
                    indices(s, s.t0 + 2 * GT)
                o, n = old[0:p, h, 0:kk, :], new[0:p, h, 0:kk, :]
                ee, pp = e[0:p, h, 0:kk, :], pw[0:p, h, 0:kk, :]
                top_old, top_new, er = o[:, :, 0:H1], n[:, :, 0:H1], o[:, :, 2 * H1 + C:STATE]
                nc.vector.tensor_tensor(ee[:, :, 0:H1], f[0:p, h, 0:kk, C:FEAT], er, ALU.add)
                merge(nc.vector.tensor_tensor(ee[:, :, H1:2 * H1], topel[0:p, h, 0:kk, :], er, ALU.add))
                merge.done()
                flat = ee.rearrange("p k j -> p (k j)")
                merge(nc.vector.scalar_tensor_tensor(flat, flat, SLOPE, flat, ALU.mult, ALU.max))
                merge.done()
                merge(nc.vector.tensor_tensor(top_new, ee[:, :, H1:2 * H1], top_old, ALU.max))
                merge.done()
                nc.vector.tensor_tensor(pp[:, :, 0:H1], ee[:, :, 0:H1], top_new, ALU.subtract)
                nc.vector.tensor_tensor(pp[:, :, H1:2 * H1], top_old, top_new, ALU.subtract).then_inc(e_ready, 1)
                dve.wait_ge(pw_ready, s.g + 1)
                nc.vector.tensor_copy(msg[0:p, h, 0:kk, 0:H1], pp[:, :, 0:H1])
                nc.vector.tensor_tensor(
                    msg[0:p, h, 0:kk, H1:H1 + C].rearrange("p k (h d) -> p k h d", d=D1),
                    f[0:p, h, 0:kk, 0:C].rearrange("p k (h d) -> p k h d", d=D1),
                    pp[:, :, 0:H1].unsqueeze(3).broadcast_to([p, kk, H1, D1]), ALU.mult).then_inc(msg_ready, 1)

            def states(s):
                p, kk, h = s.p, s.tiles, s.h
                o, n = old[0:p, h, 0:kk, :], new[0:p, h, 0:kk, :]
                pp, er = pw[0:p, h, 0:kk, :], o[:, :, 2 * H1 + C:STATE]
                fade = pp[:, :, H1:2 * H1]
                nc.vector.tensor_tensor(o[:, :, H1:2 * H1], o[:, :, H1:2 * H1], fade, ALU.mult)
                acc = o[:, :, 2 * H1:2 * H1 + C].rearrange("p k (h d) -> p k h d", d=D1)
                merge(nc.vector.tensor_tensor(acc, acc, fade.unsqueeze(3).broadcast_to([p, kk, H1, D1]), ALU.mult))
                nc.vector.tensor_copy(n[:, :, 2 * H1 + C:STATE], er)
                dve.wait_ge(summed, s.t0 + kk)
                merge.done()
                merge(nc.vector.tensor_tensor(n[:, :, H1:2 * H1 + C], ps[0:p, 0:kk, 0:H1 + C],
                                              o[:, :, H1:2 * H1 + C], ALU.add))
            pipelined(dve, rows, (1, equals), (2, powers), (0, same.vector_begin), (1, tops), (2, states))

        @block.scalar
        def _(act):
            def distance(s):
                act.wait_ge(own_p, s.g * 4 + 2)
                after(act, el_used, s.t0 - GT)
                nc.scalar.activation(far[0:s.p, s.h, 0:s.tiles, 0:s.width], same.same[0:s.p, s.h, 0:s.tiles, 0:s.width],
                                     ACT.Copy, bias=LOW, scale=-LOW).then_inc(far_ready, 1)

            def power(s):
                act.wait_ge(e_ready, s.g + 1)
                pp = pw[0:s.p, s.h, 0:s.tiles, :]
                nc.scalar.activation(pp, pp, ACT.Exp).then_inc(pw_ready, 1)
            skewed(act, rows, distance, power)


def columns_of(rows, s, table):
    if s.last:
        return table[:, rows.full * P:rows.n]
    return table[:, bass.ds(s.t0 * P, GT * P)]


def before_mlp(nc, w, c, t, rows):
    with ExitStack() as ctx:
        k_ = Kit(nc, "n2", ctx)
        B = rows.turn
        norm = Norm(nc, k_, c, B)
        x1, st = k_.sb("x1", [P, B, GT, C]), k_.sb("state", [P, B, REP, GT, STATE])
        ea = k_.sb("ea", [P, B, GT, C + 1])
        top, wt, part, total = (k_.sb("top", [P, B, GT, H1]), k_.sb("wt", [P, B, REP, GT, H1]),
                                k_.sb("part", [P, B, REP, GT, H1]), k_.sb("total", [P, B, GT, H1]))
        x2, hid, diag = k_.sb("x2", [P, B, GT, C]), k_.sb("hid", [P, B, GT, C]), k_.sb("diag", [P, B, GT, P])
        hidt, vet, z = k_.sb("hidt", [P, B, GT, P]), k_.sb("vet", [P, B, GT, P]), k_.sb("z", [P, B, GT * P])
        ps_h, ps_v, ps_z = (k_.ps(n, [P, 512]) for n in ("ps_h", "ps_v", "ps_z"))
        loaded, x2_stored, z_stored = k_.sems("loaded", B), k_.sems("x2_stored", B), k_.sems("z_stored", B)
        diff_ready, wt_ready, hid_ready = (k_.sem(n) for n in ("diff_ready", "wt_ready", "hid_ready"))
        h_ps, h_ready, v_ps, v_ready, z_ps, z_ready, z_used = (
            k_.sem(n) for n in ("h_ps", "h_ready", "v_ps", "v_ready", "z_ps", "z_ready", "z_used"))
        own_top, own_v, own_l, own_x, own_fade = (
            k_.sem(n) for n in ("own_top", "own_v", "own_l", "own_x", "own_fade"))
        loads = 16 * (2 + REP)
        TOP, CNT, SUM, X = REP - 1, 3, REP + 2, REP + 2
        block = ctx.enter_context(nc.Block())

        @block.sync
        def _(sp):
            def load(s):
                hold(sp, k_.sp_turn, own_x, (s.g - B + 1) * X + 1 if not isinstance(s.g, int) or s.g >= B else 0)
                hold(sp, k_.sp_turn, v_ps, s.g - B + 1)
                load_group(sp, rows, s, x1[:, s.h, :, :], t["x1"], 0, C, loaded[s.h])
                for r in range(REP):
                    load_group(sp, rows, s, st[:, s.h, r, :, :], t["state"][r], 0, STATE, loaded[s.h])
                load_group(sp, rows, s, ea[:, s.h, :, :], t["sums0"], C, C + 1, loaded[s.h])

            def store_x2(s):
                hold(sp, k_.sp_turn, own_x, (s.g + 1) * X + 1)
                store_group(sp, rows, s, t["x2"], x2[:, s.h, :, :], x2_stored[s.h])

            def store_z(s):
                hold(sp, k_.sp_turn, z_ready, s.g + 1)
                sp.dma_start(columns_of(rows, s, t["turned"]), z[:, s.h, 0:s.width]).then_inc(z_stored[s.h], 16)
            pipelined(sp, rows, (9, store_z), (5, store_x2), (0, load))
            stored(sp, rows, x2_stored, 1)
            stored(sp, rows, z_stored, 1)

        @block.gpsimd
        def _(pool):
            fades = Own(pool, own_fade, REP)

            def fade(s):
                p, kk, h = s.p, s.tiles, s.h
                fades.group(s)
                hold(pool, k_.pool_turn, wt_ready, s.g + 1)
                for r in range(REP):
                    f = each_head(st[0:p, h, r, 0:kk, 2 * H1:2 * H1 + C])
                    fades(nc.gpsimd.tensor_tensor(f, f, wt[0:p, h, r, 0:kk, :].unsqueeze(3).broadcast_to([p, kk, H1, D1]),
                                                  ALU.mult))
            pipelined(pool, rows, (1, fade))

        @block.tensor
        def _(pe):
            def turn_attributes(s):
                p = s.p
                pe.wait_ge(own_v, (s.g + 1) * CNT + 1)
                pe.wait_ge(loaded[s.h], s.n * loads + loads)
                after(pe, v_ready, s.g)
                for k in range(s.tiles):
                    ins = nc.tensor.matmul(ps_v[:, k * P:k * P + p], ea[0:p, s.h, k, 0:C], diag[0:p, s.h, k, 0:p],
                                           start=True, stop=True)
                ins.then_inc(v_ps, 1)

            def turn_hidden(s):
                pe.wait_ge(hid_ready, s.g + 1)
                after(pe, h_ready, s.g)
                for k in range(s.tiles):
                    ins = nc.tensor.transpose(ps_h[:, k * P:k * P + s.p], hid[0:s.p, s.h, k, :], c["ident"][0:s.p, 0:s.p])
                ins.then_inc(h_ps, 1)

            def linear(s):
                m = s.width
                pe.wait_ge(v_ready, s.g + 1)
                pe.wait_ge(h_ready, s.g + 1)
                after(pe, z_ready, s.g)
                nc.tensor.matmul(ps_z[:, 0:m], c["w0b"][:, :], vet[:, s.h, :, :].rearrange("q k p -> q (k p)")[:, 0:m],
                                 start=True, stop=False)
                nc.tensor.matmul(ps_z[:, 0:m], c["w0a"][:, :], hidt[:, s.h, :, :].rearrange("q k p -> q (k p)")[:, 0:m],
                                 start=False, stop=True).then_inc(z_ps, 1)
            pipelined(pe, rows, (6, linear), (5, turn_hidden), (1, turn_attributes))

        @block.vector
        def _(dve):
            tops, count, sums, xs = Own(dve, own_top, TOP), Own(dve, own_v, CNT), Own(dve, own_l, SUM), Own(dve, own_x, X)

            def highest(s):
                p, kk, h = s.p, s.tiles, s.h
                tops.group(s)
                dve.wait_ge(loaded[h], s.n * loads + loads)
                S, tp = st[0:p, h, :, 0:kk, :], top[0:p, h, 0:kk, :]
                tops(nc.vector.tensor_tensor(tp, S[:, 0, :, 0:H1], S[:, 1, :, 0:H1], ALU.max))
                tops.done()
                for r in range(2, REP):
                    tops(nc.vector.tensor_tensor(tp, tp, S[:, r, :, 0:H1], ALU.max))
                    tops.done()
                nc.vector.tensor_tensor(wt[0:p, h, :, 0:kk, :], S[:, :, :, 0:H1], tp.unsqueeze(1).broadcast_to([p, REP, kk, H1]),
                                        ALU.subtract).then_inc(diff_ready, 1)

            def degrees(s):
                p, kk, h = s.p, s.tiles, s.h
                count.group(s)
                dve.wait_ge(loaded[h], s.n * loads + loads)
                deg = c["rdeg"][0:p, bass.ds(s.t0, kk)]
                count(nc.vector.tensor_scalar(deg, ea[0:p, h, 0:kk, C], 1.0, None, ALU.max))
                count.done()
                dve.sem_inc(k_.dve_turn, 1)
                count(nc.vector.reciprocal(deg, deg))
                count.done()
                after(dve, v_ps, s.g - B + 1)
                count(nc.vector.tensor_tensor(diag[0:p, h, 0:kk, 0:p], c["ident"][0:p, 0:p].unsqueeze(1).broadcast_to([p, kk, p]),
                                              deg.unsqueeze(2).broadcast_to([p, kk, p]), ALU.mult))
                assert count.k == CNT

            def divisors(s):
                p, kk, h = s.p, s.tiles, s.h
                sums.group(s)
                dve.wait_ge(wt_ready, s.g + 1)
                S, Q, L = st[0:p, h, :, 0:kk, :], part[0:p, h, :, 0:kk, :], total[0:p, h, 0:kk, :]
                sums(nc.vector.tensor_tensor(Q, S[:, :, :, H1:2 * H1], wt[0:p, h, :, 0:kk, :], ALU.mult))
                sums.done()
                sums(nc.vector.tensor_tensor(L, Q[:, 0, :, :], Q[:, 1, :, :], ALU.add))
                sums.done()
                for r in range(2, REP):
                    sums(nc.vector.tensor_tensor(L, L, Q[:, r, :, :], ALU.add))
                    sums.done()
                flat = L.rearrange("p k h -> p (k h)")
                sums(nc.vector.scalar_tensor_tensor(flat, flat, 0.0, flat, ALU.is_equal, ALU.add))
                sums.done()
                sums(nc.vector.reciprocal(flat, flat))
                assert sums.k == SUM

            def residual(s):
                p, kk, h = s.p, s.tiles, s.h
                xs.group(s)
                S, A, L = st[0:p, h, :, 0:kk, 2 * H1:2 * H1 + C], x2[0:p, h, 0:kk, :], total[0:p, h, 0:kk, :]
                dve.wait_ge(own_fade, (s.g + 1) * REP + 1)
                after(dve, x2_stored[h], s.n * 16)
                xs(nc.vector.tensor_tensor(A, S[:, 0, :, :], S[:, 1, :, :], ALU.add))
                xs.done()
                for r in range(2, REP):
                    xs(nc.vector.tensor_tensor(A, A, S[:, r, :, :], ALU.add))
                    xs.done()
                dve.wait_ge(own_l, (s.g + 1) * SUM + 1)
                xs(nc.vector.tensor_tensor(each_head(A), each_head(A), L.unsqueeze(3).broadcast_to([p, kk, H1, D1]), ALU.mult))
                xs.done()
                xs(nc.vector.tensor_tensor(A, A, x1[0:p, h, 0:kk, :], ALU.add))
                xs.done()
                norm.stats(dve, xs, s, x2[:, h, :, :])
                assert xs.k == X

            def statistics(s):
                dve.wait_ge(z_ready, s.g + 1)
                dve.sem_inc(k_.dve_turn, 1)
                nc.vector.bn_stats(c["zstats"][:, bass.ds(s.g * 6, 6)], z[:, s.h, 0:s.width]).then_inc(z_used, 1)
            pipelined(dve, rows, (0, highest), (0, degrees), (2, residual), (1, divisors), (8, statistics),
                      (4, lambda s: norm.factors(dve, s)))

        @block.scalar
        def _(act):
            def power(s):
                act.wait_ge(diff_ready, s.g + 1)
                W = wt[0:s.p, s.h, :, 0:s.tiles, :].rearrange("p r k h -> p r (k h)")
                nc.scalar.activation(W, W, ACT.Exp).then_inc(wt_ready, 1)

            def copy_attributes(s):
                act.wait_ge(v_ps, s.g + 1)
                after(act, z_ps, s.g - B + 1)
                nc.scalar.activation(vet[:, s.h, 0:s.tiles, 0:s.p], across(ps_v, s), ACT.Copy).then_inc(v_ready, 1)

            def relu(s):
                after(act, h_ps, s.g - B + 1)
                norm.apply(act, s, hid[:, s.h, :, :], x2[:, s.h, :, :], hid_ready)

            def copy_hidden(s):
                act.wait_ge(h_ps, s.g + 1)
                after(act, z_ps, s.g - B + 1)
                nc.scalar.activation(hidt[:, s.h, 0:s.tiles, 0:s.p], across(ps_h, s), ACT.Copy).then_inc(h_ready, 1)

            def relu_z(s):
                act.wait_ge(z_ps, s.g + 1)
                after(act, z_used, s.g - B + 1)
                after(act, z_stored[s.h], s.n * 16)
                nc.scalar.activation(z[:, s.h, 0:s.width], ps_z[:, 0:s.width], ACT.Relu, bias=c["b0u"][:, :]).then_inc(z_ready, 1)

            def root(s, early):
                if early == ((s.h + 3) % B % 2 == 0):
                    norm.root(act, s)
            pipelined(act, rows, (5, relu), (7, relu_z), (6, copy_hidden), (2, copy_attributes),
                      (3, lambda s: root(s, True)), (0, power), (3, lambda s: root(s, False)))



def batch_norm(nc, c, rows, layer):
    gamma, beta = c[f"g{layer}"], c[f"t{layer}"]
    following = {0: ("w1", "b1"), 1: ("w2", "b2")}.get(layer)
    with ExitStack() as ctx:
        k_ = Kit(nc, f"bn{layer}", ctx)
        mv, sd, neg = k_.sb("mv", [P, 2]), k_.sb("sd", [P, 1]), k_.sb("neg", [P, 1])
        ps = k_.ps("ps", [P, 512])
        own, var_ready, sd_ready, shift_ready, product = (
            k_.sem(n) for n in ("own", "var_ready", "sd_ready", "shift_ready", "product"))
        block = ctx.enter_context(nc.Block())

        @block.vector
        def _(dve):
            nc.vector.bn_aggr(mv[:, :], c["zstats"][:, :]).then_inc(var_ready, 1)
            dve.wait_ge(sd_ready, 1)
            nc.vector.reciprocal(sd[:, :], sd[:, :]).then_inc(own, 1)
            dve.wait_ge(own, 1)
            nc.vector.tensor_tensor(c["scale"][:, :], gamma[:, :], sd[:, :], ALU.mult).then_inc(own, 1)
            dve.wait_ge(own, 2)
            nc.vector.scalar_tensor_tensor(neg[:, :], mv[:, 0:1], -1.0, c["scale"][:, :], ALU.mult, ALU.mult).then_inc(own, 1)
            dve.wait_ge(own, 3)
            nc.vector.tensor_tensor(c["shift"][:, :], neg[:, :], beta[:, :], ALU.add).then_inc(shift_ready, 1)
            if following:
                weight, bias = c[following[0]], c[following[1]]
                nc.vector.tensor_scalar(c["wnext"][:, :], weight[:, :], c["scale"][:, :], None, ALU.mult)
                dve.wait_ge(product, 1)
                nc.vector.tensor_tensor(c["bnext"][:, :], ps[:, 0:1], bias[:, :], ALU.add)

        @block.scalar
        def _(act):
            act.wait_ge(var_ready, 1)
            nc.scalar.activation(sd[:, :], mv[:, 1:2], ACT.Sqrt, bias=c["eps"][:, :]).then_inc(sd_ready, 1)

        if following:
            @block.tensor
            def _(pe):
                pe.wait_ge(shift_ready, 1)
                nc.tensor.matmul(ps[:, 0:1], c[following[0]][:, :], c["shift"][:, :], start=True, stop=True).then_inc(product, 1)


def mlp_layer(nc, c, source, target, rows, layer):
    with ExitStack() as ctx:
        k_ = Kit(nc, f"mlp{layer}", ctx)
        B = rows.turn
        z, y = k_.sb("z", [P, B, GT * P]), k_.sb("y", [P, B, GT * P])
        ps = k_.ps("ps", [P, B, 512])
        loaded, y_stored = k_.sems("loaded", B), k_.sems("y_stored", B)
        product, y_ready, counted = k_.sem("product"), k_.sem("y_ready"), k_.sem("counted")
        block = ctx.enter_context(nc.Block())

        @block.sync
        def _(sp):
            def load(s):
                hold(sp, k_.sp_turn, product, s.g - B + 1)
                sp.dma_start(z[:, s.h, 0:s.width], columns_of(rows, s, source)).then_inc(loaded[s.h], 16)
            pipelined(sp, rows, (0, load))

        @block.tensor
        def _(pe):
            def multiply(s):
                pe.wait_ge(loaded[s.h], s.n * 16 + 16)
                after(pe, y_ready, s.g - B + 1)
                nc.tensor.matmul(ps[:, s.h, 0:s.width], c["wnext"][:, :], z[:, s.h, 0:s.width],
                                 start=True, stop=True).then_inc(product, 1)
            pipelined(pe, rows, (0, multiply))

        @block.scalar
        def _(act):
            def store(s):
                act.wait_ge(y_ready, s.g + 1)
                act.dma_start(columns_of(rows, s, target), y[:, s.h, 0:s.width]).then_inc(y_stored[s.h], 16)

            def relu(s):
                act.wait_ge(product, s.g + 1)
                after(act, counted, s.g - B + 1)
                after(act, y_stored[s.h], s.n * 16)
                nc.scalar.activation(y[:, s.h, 0:s.width], ps[:, s.h, 0:s.width], ACT.Relu,
                                     bias=c["bnext"][:, :]).then_inc(y_ready, 1)
            pipelined(act, rows, (0, relu), (1, store))
            stored(act, rows, y_stored, 1)

        @block.vector
        def _(dve):
            def count(s):
                dve.wait_ge(y_ready, s.g + 1)
                dve.sem_inc(k_.dve_turn, 1)
                nc.vector.bn_stats(c["zstats"][:, bass.ds(s.g * 6, 6)], y[:, s.h, 0:s.width]).then_inc(counted, 1)
            pipelined(dve, rows, (0, count))


def after_mlp(nc, c, t, rows):
    with ExitStack() as ctx:
        k_ = Kit(nc, "n5", ctx)
        B = rows.turn
        norm = Norm(nc, k_, c, B)
        z, y = k_.sb("z", [P, B, GT * P]), k_.sb("y", [P, B, GT * P])
        x2, x3, x3b, hid = (k_.sb(n, [P, B, GT, C]) for n in ("x2", "x3", "x3b", "hid"))
        ps = k_.ps("ps", [P, 512])
        loaded, done = k_.sems("loaded", B), k_.sems("stored", B)
        own, y_ready, turned, hid_ready, biased = (k_.sem(n) for n in ("own", "y_ready", "turned", "hid_ready", "biased"))
        block = ctx.enter_context(nc.Block())

        @block.sync
        def _(sp):
            def load(s):
                hold(sp, k_.sp_turn, own, (s.g - B) * 2 + 2)
                hold(sp, k_.sp_turn, y_ready, s.g - B + 1)
                sp.dma_start(z[:, s.h, 0:s.width], columns_of(rows, s, t["turned"])).then_inc(loaded[s.h], 16)
                load_group(sp, rows, s, x2[:, s.h, :, :], t["x2"], 0, C, loaded[s.h])

            def store(s):
                hold(sp, k_.sp_turn, hid_ready, s.g + 1)
                hold(sp, k_.sp_turn, biased, s.g + 1)
                store_group(sp, rows, s, t["x3"], x3b[:, s.h, :, :], done[s.h])
                store_group(sp, rows, s, t["h3"], hid[:, s.h, :, :], done[s.h])
            pipelined(sp, rows, (8, store), (0, load))
            stored(sp, rows, done, 2)

        @block.scalar
        def _(act):
            def normalise(s):
                act.wait_ge(loaded[s.h], s.n * 32 + 32)
                after(act, turned, s.g - B + 1)
                nc.scalar.activation(y[:, s.h, 0:s.width], z[:, s.h, 0:s.width], ACT.Identity, bias=c["shift"][:, :],
                                     scale=c["scale"][:, :]).then_inc(y_ready, 1)

            def relu(s):
                after(act, done[s.h], s.n * 32)
                norm.apply(act, s, hid[:, s.h, :, :], x3[:, s.h, :, :], hid_ready)
            pipelined(act, rows, (0, normalise), (5, relu), (3, lambda s: norm.root(act, s)))

        @block.tensor
        def _(pe):
            def turn(s):
                pe.wait_ge(y_ready, s.g + 1)
                after(pe, own, (s.g - 1) * 2 + 2)
                for k in range(s.tiles):
                    ins = nc.tensor.transpose(ps[0:s.p, k * C:(k + 1) * C], y[:, s.h, k * P:k * P + s.p], c["ident"][:, :])
                ins.then_inc(turned, 1)
            pipelined(pe, rows, (0, turn))

        @block.vector
        def _(dve):
            mine = Own(dve, own, 2)

            def residual(s):
                p, kk = s.p, s.tiles
                mine.group(s)
                dve.wait_ge(turned, s.g + 1)
                after(dve, biased, s.g - B + 1)
                after(dve, hid_ready, s.g - B + 1)
                mine(nc.vector.tensor_tensor(x3[0:p, s.h, 0:kk, :], tiles_in(ps, s), x2[0:p, s.h, 0:kk, :], ALU.add))
                mine.done()
                norm.stats(dve, mine, s, x3[:, s.h, :, :])
            pipelined(dve, rows, (1, residual), (4, lambda s: norm.factors(dve, s)))

        @block.gpsimd
        def _(pool):
            def bias(s):
                p, kk = s.p, s.tiles
                hold(pool, k_.pool_turn, own, s.g * 2 + 2)
                hold(pool, k_.pool_turn, done[s.h], s.n * 32)
                nc.gpsimd.tensor_tensor(x3b[0:p, s.h, 0:kk, :], x3[0:p, s.h, 0:kk, :],
                                        c["b3"][0:p, :].unsqueeze(1).broadcast_to([p, kk, C]), ALU.add).then_inc(biased, 1)
            pipelined(pool, rows, (2, bias))


def last_linear(nc, c, t, out, rows):
    with ExitStack() as ctx:
        k_ = Kit(nc, "n6", ctx)
        B = rows.turn
        x3, hid = k_.sb("x3", [P, B, GT, C]), k_.sb("hid", [P, B, GT, C])
        a, diag = k_.sb("a", [P, B, GT, C]), k_.sb("diag", [P, B, GT, P])
        hidt, at, y = k_.sb("hidt", [P, B, GT, P]), k_.sb("at", [P, B, GT, P]), k_.sb("y", [P, B, GT, C])
        ps_h, ps_a, ps_y = (k_.ps(n, [P, 512]) for n in ("ps_h", "ps_a", "ps_y"))
        loaded, done = k_.sems("loaded", B), k_.sems("stored", B)
        diag_ready, h_ps, a_ps, h_ready, a_ready, y_ps, y_ready = (
            k_.sem(n) for n in ("diag_ready", "h_ps", "a_ps", "h_ready", "a_ready", "y_ps", "y_ready"))
        loads = 16 * 3
        block = ctx.enter_context(nc.Block())

        @block.sync
        def _(sp):
            def load(s):
                hold(sp, k_.sp_turn, a_ps, s.g - B + 1)
                hold(sp, k_.sp_turn, h_ps, s.g - B + 1)
                hold(sp, k_.sp_turn, y_ready, s.g - B + 1)
                load_group(sp, rows, s, x3[:, s.h, :, :], t["x3"], 0, C, loaded[s.h])
                load_group(sp, rows, s, hid[:, s.h, :, :], t["h3"], 0, C, loaded[s.h])
                load_group(sp, rows, s, a[:, s.h, :, :], t["sums3"], 0, C, loaded[s.h])

            def store(s):
                hold(sp, k_.sp_turn, y_ready, s.g + 1)
                store_group(sp, rows, s, out, y[:, s.h, :, :], done[s.h])
            pipelined(sp, rows, (5, store), (0, load))
            stored(sp, rows, done, 1)

        @block.tensor
        def _(pe):
            def turn_hidden(s):
                pe.wait_ge(loaded[s.h], s.n * loads + loads)
                after(pe, h_ready, s.g)
                for k in range(s.tiles):
                    ins = nc.tensor.transpose(ps_h[:, k * P:k * P + s.p], hid[0:s.p, s.h, k, :], c["ident"][0:s.p, 0:s.p])
                ins.then_inc(h_ps, 1)

            def turn_means(s):
                p = s.p
                pe.wait_ge(loaded[s.h], s.n * loads + loads)
                pe.wait_ge(diag_ready, s.g + 1)
                after(pe, a_ready, s.g)
                for k in range(s.tiles):
                    ins = nc.tensor.matmul(ps_a[:, k * P:k * P + p], a[0:p, s.h, k, :], diag[0:p, s.h, k, 0:p],
                                           start=True, stop=True)
                ins.then_inc(a_ps, 1)

            def linear(s):
                p = s.p
                pe.wait_ge(h_ready, s.g + 1)
                pe.wait_ge(a_ready, s.g + 1)
                after(pe, y_ready, s.g)
                for k in range(s.tiles):
                    to = ps_y[0:p, k * C:(k + 1) * C]
                    nc.tensor.matmul(to, hidt[:, s.h, k, 0:p], c["w3a"][:, :], start=True, stop=False)
                    ins = nc.tensor.matmul(to, at[:, s.h, k, 0:p], c["w3b"][:, :], start=False, stop=True)
                ins.then_inc(y_ps, 1)
            pipelined(pe, rows, (3, linear), (1, turn_means), (1, turn_hidden))

        @block.scalar
        def _(act):
            def copies(s):
                for got, src, dst, sem in ((a_ps, ps_a, at, a_ready), (h_ps, ps_h, hidt, h_ready)):
                    act.wait_ge(got, s.g + 1)
                    after(act, y_ps, s.g - B + 1)
                    nc.scalar.activation(dst[:, s.h, 0:s.tiles, 0:s.p], across(src, s), ACT.Copy).then_inc(sem, 1)
            pipelined(act, rows, (2, copies))

        @block.vector
        def _(dve):
            def diagonal(s):
                p, kk, h = s.p, s.tiles, s.h
                after(dve, a_ps, s.g - B + 1)
                nc.vector.tensor_tensor(diag[0:p, h, 0:kk, 0:p], c["ident"][0:p, 0:p].unsqueeze(1).broadcast_to([p, kk, p]),
                                        c["rdeg"][0:p, bass.ds(s.t0, kk)].unsqueeze(2).broadcast_to([p, kk, p]),
                                        ALU.mult).then_inc(diag_ready, 1)

            def residual(s):
                p, kk, h = s.p, s.tiles, s.h
                dve.wait_ge(y_ps, s.g + 1)
                after(dve, done[h], s.n * 16)
                nc.vector.tensor_tensor(y[0:p, h, 0:kk, :], tiles_in(ps_y, s), x3[0:p, h, 0:kk, :], ALU.add).then_inc(y_ready, 1)
            pipelined(dve, rows, (3, residual), (0, diagonal))


def clear_scores(nc, scores, rows):
    with ExitStack() as ctx:
        block = ctx.enter_context(nc.Block())

        @block.vector
        def _(dve):
            nc.vector.memset(scores[:, rows.full:rows.full + 1, :], LOW)


def gnn_kernel(nc, w, out):
    n = w["x"].shape[0]
    rows, nodes = Rows(n, 2), Rows(n, 5)
    T = rows.full + 1
    with ExitStack() as ctx:
        Kit.shared = [ctx.enter_context(nc.semaphore(f"soft_{i}")) for i in range(2 * GT)]
        k_ = Kit(nc, "all", ctx)
        c = {name: k_.sb(name, shape) for name, shape in {
            "ident": [P, P], "lower": [P, GT * P], "eps": [P, 1], "spare": [P, GT],
            "wq": [P, C + H0], "wkv": [P, 2 * C + H0], "wo": [P, C], "wfeat": [P, C + 2 * H1],
            "w0a": [P, C], "w0b": [P, C], "w1": [P, C], "w2": [P, C], "w3a": [P, C], "w3b": [P, C],
            "bo": [P, C], "b3": [P, C], "bqb": [P, C], "bkvb": [P, 2 * C], "bd": [P, H0], "wdraw": [P, H0],
            "b0": [P, 1], "b1": [P, 1], "b2": [P, 1], "g0": [P, 1], "g1": [P, 1], "g2": [P, 1],
            "t0": [P, 1], "t1": [P, 1], "t2": [P, 1], "b0u": [P, 1], "rdeg": [P, T],
            "zstats": [P, 6 * (rows.groups + 1)], "scale": [P, 1], "shift": [P, 1],
            "wnext": [P, C], "bnext": [P, 1]}.items()}
        c["spare_i"] = k_.sb("spare_i", [P, GT], I32)
        tables = {"v": k_.dram("v", [n, C]), "x1": k_.dram("x1", [n, C]), "x2": k_.dram("x2", [n, C]),
                  "x3": k_.dram("x3", [n, C]), "h3": k_.dram("h3", [n, C]), "feat": k_.dram("feat", [n, FEAT]),
                  "turned": k_.dram("turned", [C, n]), "turned2": k_.dram("turned2", [C, n]),
                  "state": [k_.dram(f"state_{r}", [n + GT * P, STATE]) for r in range(REP)],
                  "sums0": k_.dram("sums0", [n + GT * P, MSG]), "sums3": k_.dram("sums3", [n + GT * P, C])}
        prepare(nc, w, c, tables, rows)
        with ExitStack() as inner:
            scores = Kit(nc, "edge", inner).sb("scores", [P, T, H0])
            clear_scores(nc, scores, rows)
            edge_scores(nc, w, c, tables, rows, scores)
            edge_weights(nc, c, rows, scores)
            add_by_source(nc, w, c, tables, rows, scores, 0)
        after_attention(nc, w, c, tables, nodes)
        add_by_target(nc, w, c, tables, rows)
        before_mlp(nc, w, c, tables, nodes)
        batch_norm(nc, c, rows, 0)
        mlp_layer(nc, c, tables["turned"], tables["turned2"], nodes, 1)
        batch_norm(nc, c, rows, 1)
        mlp_layer(nc, c, tables["turned2"], tables["turned"], nodes, 2)
        batch_norm(nc, c, rows, 2)
        after_mlp(nc, c, tables, nodes)
        add_by_source(nc, w, c, tables, rows, None, 3)
        last_linear(nc, c, tables, out, nodes)


_INS = ["x", "src", "dst", "edge_attr_128", "edge_weight",
        "L0_gnn_Wq", "L0_gnn_bq", "L0_gnn_Wk", "L0_gnn_bk", "L0_gnn_Wv", "L0_gnn_bv", "L0_gnn_Wd", "L0_gnn_bd",
        "L0_gnn_Wo", "L0_gnn_bo", "L1_gnn_W", "L1_gnn_attn_l", "L1_gnn_attn_r", "L2_gnn_u", "L2_gnn_W0",
        "L2_gnn_b0", "L2_gnn_W1", "L2_gnn_b1", "L2_gnn_W2", "L2_gnn_b2", "L2_gnn_g0", "L2_gnn_beta0",
        "L2_gnn_g1", "L2_gnn_beta1", "L2_gnn_g2", "L2_gnn_beta2", "L3_gnn_W", "L3_gnn_b"]


def kernel(**inputs):
    import numpy as _np
    import concourse.bacc as _bacc
    from concourse import mybir as _mybir
    from concourse.bass_utils import run_bass_kernel_spmd as _run

    nc = _bacc.Bacc("TRN2", target_bir_lowering=False, num_devices=1)
    arrays, args = {}, {}
    for name in _INS:
        a = _np.ascontiguousarray(inputs[name])
        arrays[f"in_{name}_dram"] = a
        args[name] = nc.dram_tensor(f"in_{name}_dram", a.shape, _mybir.dt.from_np(a.dtype), kind="ExternalInput").ap()
    out = nc.dram_tensor("out_0_dram", inputs["x"].shape, _mybir.dt.float32, kind="ExternalOutput").ap()
    gnn_kernel(nc, args, out)
    r = _run(nc, [arrays], core_ids=[0])
    return r.results[0]["out_0_dram"]
```
